# Optimizing a Trainium2 kernel written in Bass

```python
import numpy as np
import jax
import jax.numpy as jnp

def _softmax(x, axis=-1):
    return jax.nn.softmax(x, axis=axis)

def _gelu(x):
    return jax.nn.gelu(x, approximate=True)

def _silu(x):
    return jax.nn.silu(x)

def _sigmoid(x):
    return jax.nn.sigmoid(x)

def _layernorm(x, axis=-1, eps=1e-05):
    m = jnp.mean(x, axis=axis, keepdims=True)
    v = jnp.var(x, axis=axis, keepdims=True)
    return (x - m) / jnp.sqrt(v + eps)

def _scatter_add(tgt, idx, src, axis=0):
    return tgt.at[idx].add(src)

def _segment_sum(src, seg, n):
    return jax.ops.segment_sum(src, seg, n)
kernel_name = 'mk_sandwich_d1_jaxref_r4_cb061b'

def setup_inputs(seed: int=0):
    np.random.seed(seed)
    _w = jnp.asarray

    def _L0_attn_setup():
        import jax, jax.numpy as jnp
        import numpy as np
        import math
        DIM = 256
        HEADS = 16
        HEAD_DIM = DIM // HEADS
        B, N = (1, 1024)
        key = jax.random.key(seed)
        k1, k2, k3, k4 = jax.random.split(key, 4)
        content = jax.random.normal(k1, (B, N, DIM), dtype=jnp.float32)
        Wq = jnp.eye(DIM, dtype=jnp.float32) + 0.02 * jax.random.normal(k2, (DIM, DIM), dtype=jnp.float32)
        Wk = jnp.eye(DIM, dtype=jnp.float32) + 0.02 * jax.random.normal(k3, (DIM, DIM), dtype=jnp.float32)
        Wv = jnp.eye(DIM, dtype=jnp.float32) + 0.02 * jax.random.normal(k4, (DIM, DIM), dtype=jnp.float32)
        return {'content': content, 'Wq': Wq, 'Wk': Wk, 'Wv': Wv}
    _L0_attn_in = _L0_attn_setup()

    def _L0_ffn_setup():
        import jax, jax.numpy as jnp
        import numpy as np
        B, S, D = (4, 512, 256)
        E, K = (8, 2)
        DFF = 4 * D
        key = jax.random.key(seed)
        k1, k2, k3, k4 = jax.random.split(key, 4)
        x = jax.random.normal(k1, (B, S, D), dtype=jnp.float32)
        router_w = jax.random.normal(k2, (D, E), dtype=jnp.float32) * (1.0 / np.sqrt(D))
        w_fc = jax.random.normal(k3, (E, D, DFF), dtype=jnp.float32) * (1.0 / np.sqrt(D))
        w_proj = jax.random.normal(k4, (E, DFF, D), dtype=jnp.float32) * (1.0 / np.sqrt(DFF))
        return {'x': x, 'router_w': router_w, 'w_fc': w_fc, 'w_proj': w_proj}
    _L0_ffn_in = _L0_ffn_setup()
    _d = {'L0_attn_content': _L0_attn_in['content'], 'L0_attn_Wq': _L0_attn_in['Wq'], 'L0_attn_Wk': _L0_attn_in['Wk'], 'L0_attn_Wv': _L0_attn_in['Wv'], 'L0_ffn_router_w': _L0_ffn_in['router_w'], 'L0_ffn_w_fc': _L0_ffn_in['w_fc'], 'L0_ffn_w_proj': _L0_ffn_in['w_proj']}
    _x0 = _d['L0_attn_content']
    _d['L0_attn_content'] = jax.random.normal(jax.random.fold_in(jax.random.key(seed), 1), (4, 1024, 256), dtype=_x0.dtype)
    del _x0
    return _d

def reference(L0_attn_content, L0_attn_Wq, L0_attn_Wk, L0_attn_Wv, L0_ffn_router_w, L0_ffn_w_fc, L0_ffn_w_proj):

    def _L0_attn_ref(content, Wq, Wk, Wv):
        import jax, jax.numpy as jnp
        import numpy as np
        import math
        DIM = 256
        HEADS = 16
        HEAD_DIM = DIM // HEADS
        B, N = (1, 1024)
        b, n, d = content.shape
        Q = (content @ Wq).reshape(b, n, HEADS, HEAD_DIM)
        K = (content @ Wk).reshape(b, n, HEADS, HEAD_DIM)
        V = (content @ Wv).reshape(b, n, HEADS, HEAD_DIM)
        scores = jnp.einsum('bqhd,bkhd->bhqk', Q, K) / math.sqrt(HEAD_DIM)
        alpha = jax.nn.softmax(scores, axis=-1)
        causal = jnp.tril(jnp.ones((n, n), dtype=bool))
        alpha = jnp.where(causal, alpha, jnp.zeros((), dtype=alpha.dtype))
        Y = jnp.einsum('bhqk,bkhd->bqhd', alpha, V).reshape(b, n, d)
        return Y

    def _L0_ffn_ref(x, router_w, w_fc, w_proj):
        import jax, jax.numpy as jnp
        import numpy as np
        B, S, D = (4, 512, 256)
        E, K = (8, 2)
        DFF = 4 * D
        b, s, d = x.shape
        flat_x = x.reshape(b * s, d)
        router_logits = flat_x @ router_w
        router_probs = jax.nn.softmax(router_logits, axis=-1)
        topk_w, topk_idx = jax.lax.top_k(router_probs, K)
        topk_w = topk_w / jnp.sum(topk_w, axis=-1, keepdims=True)
        combine = jnp.sum(jax.nn.one_hot(topk_idx, E, dtype=flat_x.dtype) * topk_w[..., None], axis=1)
        out = jnp.zeros_like(flat_x)
        for e in range(E):
            h = jax.nn.gelu(flat_x @ w_fc[e], approximate=False)
            out = out + combine[:, e:e + 1] * (h @ w_proj[e])
        return out.reshape(b, s, d)
    x = L0_attn_content
    x = x + _layernorm(_L0_attn_ref(_layernorm(x, axis=-1), L0_attn_Wq, L0_attn_Wk, L0_attn_Wv), axis=-1)
    x = x + _layernorm(_L0_ffn_ref(_layernorm(x, axis=-1), L0_ffn_router_w, L0_ffn_w_fc, L0_ffn_w_proj), axis=-1)
    return x

_drawn_inputs = setup_inputs


def setup_inputs(seed=0):
    import zlib

    import numpy as np

    out = dict(_drawn_inputs(seed))
    spreads = {}
    factors = {}
    for name, (base, spread) in spreads.items():
        noise = np.random.default_rng([zlib.crc32(name.encode()), seed]).standard_normal(out[name].shape)
        drawn = base * np.exp(spread * noise) if base else spread * noise
        out[name] = jnp.asarray(drawn.astype(out[name].dtype))
    for name, factor in factors.items():
        out[name] = (out[name] * factor).astype(out[name].dtype)
    return out
```

```python
import concourse.bass as bass
from concourse import mybir
from contextlib import ExitStack


def sandwich(nc, x_d, wq_d, wk_d, wv_d, router_d, wfc_d, wproj_d, out_d):
    F32, BF16, I32, U32 = mybir.dt.float32, mybir.dt.bfloat16, mybir.dt.int32, mybir.dt.uint32
    ACT = mybir.ActivationFunctionType
    ALU = mybir.AluOpType
    AX = mybir.AxisListType
    ds = bass.ds

    P = 128
    NB, N, D = x_d.shape
    H, DH = 16, D // 16
    KC = D // P
    QT = N // P
    NH = NB * H
    TT = NB * QT
    E, _, FF = wfc_d.shape
    FC = FF // P
    TOPK = 2
    NT = TT * TOPK + E - 1
    CT = 512
    TPC = CT // P
    CPB = N // CT
    TERMS = 6
    SROWS = TERMS * DH
    Q_SCALE = DH ** -0.5
    EPS = 1e-5
    WSTEP = KC * FF
    assert WSTEP == FC * D and CPB == 2 and N == 1024

    qk_d = nc.dram_tensor("qk_parts", [2, 3, NB * D, N], BF16, kind="Internal").ap()
    xs_d = nc.dram_tensor("expert_in", [NT * P, D], F32, kind="Internal").ap()
    ys_d = nc.dram_tensor("expert_out", [NT * P, D], F32, kind="Internal").ap()

    x_t = x_d.rearrange("b (i p) d -> p (b i) d", p=P)
    out_t = out_d.rearrange("b (i p) d -> p (b i) d", p=P)

    ctx = ExitStack()
    with ctx:
        def sb(name, shape, dt=F32):
            return ctx.enter_context(nc.sbuf_tensor(name, shape, dt))

        def sem(name):
            return ctx.enter_context(nc.semaphore(name))

        wfc = sb("wfc", [P, E * WSTEP])
        arena = sb("arena", [P, E * WSTEP])
        yx = sb("yx", [P, TT, D])
        x1 = sb("x1", [P, TT, D])

        KB = 256
        v_sb = arena[:, 0:NH * QT * DH]
        a0 = NH * QT * DH
        qs = [arena[:, a0 + s * 2 * KB:a0 + (s + 1) * 2 * KB].bitcast(BF16) for s in range(2)]
        a0 += 4 * KB
        ks = [arena[:, a0 + s * 2 * KB:a0 + (s + 1) * 2 * KB].bitcast(BF16) for s in range(2)]
        a0 += 4 * KB
        e_sb = [arena[:, a0 + s * N:a0 + (s + 1) * N] for s in range(4)]
        a0 += 4 * N
        et_sb = [arena[:, a0 + s * N:a0 + (s + 1) * N] for s in range(2)]
        a0 += 2 * N
        assert a0 <= E * WSTEP

        yx_f = yx[:, :, :].rearrange("p t d -> p (t d)")
        x1_f = x1[:, :, :].rearrange("p t d -> p (t d)")
        if NB == 4:
            pa, pb = yx_f, x1_f
        else:
            pa = sb("pa", [P, 22 * KB])[:, :]
            pb = sb("pb", [P, 16 * KB])[:, :]
        xc = [pa[:, s * TPC * D:(s + 1) * TPC * D].rearrange("p (t d) -> p t d", d=D) for s in range(2)]
        o = 2 * TPC * D
        xnT = [pa[:, o + s * KC * CT:o + (s + 1) * KC * CT].rearrange("p (k t) -> p k t", k=KC) for s in range(2)]
        o += 2 * KC * CT
        wqkv = pa[:, o:o + 3 * KC * D].rearrange("p (w k d) -> p w k d", w=3, k=KC)
        parts = [pb[:, g * 3 * KB:(g + 1) * 3 * KB].bitcast(BF16).rearrange("p (s t) -> p s t", s=3)
                 for g in range(4)]
        o = 12 * KB
        resid = [pb[:, o + s * CT:o + (s + 1) * CT] for s in range(2)]

        ident = sb("ident", [P, P])
        stats = sb("stats", [P, 2, TPC, 6])
        mv = sb("mv", [P, 2, TPC, 2])
        std = sb("std", [P, 2, TPC])
        rstd = sb("rstd", [P, 2, TPC])
        negmax = sb("negmax", [P, 2, QT])
        den = sb("den", [P, 2, QT])
        rden = sb("rden", [P, 2, QT])
        warm = sb("warm", [P, 2])
        pause = sb("pause", [P, 1])
        causal = sb("causal", [P, P])
        cst0 = sb("cst0", [P, 1])
        router = sb("router", [P, KC, E])
        lg = sb("lg", [P, TT, E])
        top = sb("top", [P, TT, 8])
        topi = sb("topi", [P, TT, 8], U32)
        choice = sb("choice", [P, TOPK, TT])
        oh = sb("oh", [P, TOPK, TT, E])
        oh_bf = sb("oh_bf", [P, TT, E], BF16)
        gate = sb("gate", [P, TOPK, TT])
        gtmp = sb("gtmp", [P, TT])
        iota_e = sb("iota_e", [P, E])
        lower = sb("lower", [P, P], BF16)
        ones = sb("ones", [P, P], BF16)
        thr = sb("thr", [P, TT])
        cnt = sb("cnt", [P, E])
        ntile = sb("ntile", [P, E])
        tle = sb("tle", [P, E, E])
        endt = sb("endt", [P, E])
        base = sb("base", [P, E])
        posf = sb("posf", [P, TOPK, TT])
        pos = sb("pos", [P, TOPK, TT], I32)
        iota_t = sb("iota_t", [1, NT])
        tabf = sb("tabf", [1, NT])
        tab = sb("tab", [1, NT], I32)
        x2T = sb("x2T", [P, KC, CT])
        zero = x2T[:, 0, 0:D]
        tmp_e = sb("tmp_e", [P, E, E])
        x2T_f = x2T[:, :, :].rearrange("p k t -> p (k t)")
        tmp = x2T_f[:, 0:TT * E].rearrange("p (t e) -> p t e", e=E)
        tmp_t = x2T_f[:, TT * E:2 * TT * E].rearrange("p (e t) -> p e t", e=E)
        tmp_n = x2T_f[0:1, 0:NT * E].rearrange("p (t e) -> p t e", e=E)

        NG = 4
        ym = yx_f if NB == 4 else pa
        o = 0

        def piece(n):
            nonlocal o
            o += n
            return ym[:, o - n:o]

        xslot = [piece(D) for _ in range(2)]
        yslot = [piece(D) for _ in range(2)]
        hid = piece(FF)
        hidT = piece(FF).rearrange("p (c t) -> p c t", c=FC)
        xsT = piece(KC * P).rearrange("p (k t) -> p k t", k=KC)
        ct = [piece(2 * D).rearrange("p (j d) -> p j d", j=2) for _ in range(NG)]

        ps = ctx.enter_context(nc.psum_tensor("ps", [P, 8, 512], F32))

        def bk(i):
            return ps[:, i, :]

        s_w = sem("s_w")
        s_ident = sem("s_ident")
        s_const = sem("s_const")
        s_x = [sem("s_x0"), sem("s_x1")]
        s_bn = sem("s_bn")
        s_var = sem("s_var")
        s_std = sem("s_std")
        s_xn = sem("s_xn")
        s_xt = sem("s_xt")
        s_xta = sem("s_xta")
        s_xtd = sem("s_xtd")
        s_qk = sem("s_qk")
        s_p1 = sem("s_p1")
        s_res = sem("s_res")
        s_p2 = sem("s_p2")
        s_p3 = sem("s_p3")
        s_st = [sem(f"s_st{g}") for g in range(4)]
        s_v = sem("s_v")
        s_ve = sem("s_ve")
        s_wfc = sem("s_wfc")
        s_ld = [sem("s_ld0"), sem("s_ld1")]
        s_S = sem("s_S")
        s_max = sem("s_max")
        s_exp = sem("s_exp")
        s_mask = sem("s_mask")
        s_T = sem("s_T")
        s_evA = sem("s_evA")
        s_evD = sem("s_evD")
        s_pv = sem("s_pv")
        s_rc = sem("s_rc")
        s_norm = sem("s_norm")
        s_zero = sem("s_zero")
        s_xsz = sem("s_xsz")
        s_xin = sem("s_xin")
        s_wp = sem("s_wp")
        s_bn2 = sem("s_bn2")
        s_var2 = sem("s_var2")
        s_std2 = sem("s_std2")
        s_y2 = sem("s_y2")
        s_add = sem("s_add")
        s_x2 = sem("s_x2")
        s_x2t = sem("s_x2t")
        s_x2e = sem("s_x2e")
        s_lg = sem("s_lg")
        s_r = sem("s_r")
        s_d2 = sem("s_d2")
        s_ex2 = sem("s_ex2")
        s_oh = sem("s_oh")
        s_rank = sem("s_rank")
        s_pos = sem("s_pos")
        s_tab = sem("s_tab")
        s_sc = sem("s_sc")
        s_xs = [sem("s_xs0"), sem("s_xs1")]
        s_mt = sem("s_mt")
        s_me = sem("s_me")
        s_fc = sem("s_fc")
        s_ge = sem("s_ge")
        s_ht = sem("s_ht")
        s_hea = sem("s_hea")
        s_hed = sem("s_hed")
        s_pr = sem("s_pr")
        s_yo = sem("s_yo")
        s_ys = [sem("s_ys0"), sem("s_ys1")]
        s_g = [sem(f"s_g{i}") for i in range(NG)]
        s_cc = sem("s_cc")
        s_var3 = sem("s_var3")
        s_std3 = sem("s_std3")
        s_o = sem("s_o")
        s_out = [sem(f"s_out{i}") for i in range(NG)]
        s_warm = sem("s_warm")

        block = ctx.enter_context(nc.Block())

        BPC = 4
        DVE_CHUNKS = {(0, 0), (1, 0), (4, 1), (5, 1), (6, 1)}
        chunks = []
        nd = na = 0
        for i in range(QT):
            for c in range((i + 1 + BPC - 1) // BPC):
                chunks.append((i, c, min(BPC, i + 1 - BPC * c), len(chunks), nd, na))
                if (i, c) in DVE_CHUNKS:
                    nd += 1
                else:
                    na += 1
        NC, ND, NA = len(chunks), nd, na
        assert NC % 2 == 0
        of_unit = {i: [ch for ch in chunks if ch[0] == i] for i in range(QT)}
        LAG_T, LAG_V, LAG_N = 2, 3, 4
        LAG_E = LAG_T
        PAIR = 2 * QT
        NP = NH // 2

        def unit(k):
            return k // QT, k % QT

        def wait_pos(eng, s, v):
            if isinstance(v, int) and v <= 0:
                return
            eng.wait_ge(s, v)

        def count_T(k):
            hl, i = unit(k)
            last = of_unit[i][-1]
            return NC * hl + last[3] + 1

        def copied(eng, p, hl, n):
            if n < 0:
                hl, n = hl - 1, n + NC
            if isinstance(p, int) and 2 * p + hl < 0:
                return
            i, c, _, _, n_d, n_a = chunks[n]
            if (i, c) in DVE_CHUNKS:
                eng.wait_ge(s_evD, (2 * p + hl) * ND + n_d + 1)
            else:
                eng.wait_ge(s_evA, (2 * p + hl) * NA + n_a + 1)

        def copies(eng, p, k, by_dve, first, tail):
            k2 = k - LAG_T
            if (first and k2 < 0) or (tail and k2 >= 0):
                return
            hl, i = unit(k2)
            for (_, c, nblk, n, _, _) in of_unit[i]:
                if ((i, c) in DVE_CHUNKS) != by_dve:
                    continue
                eng.wait_ge(s_T, (2 * p + hl) * NC + n + 1)
                wait_pos(eng, s_pv, PAIR * p + k2 - 1)
                dst = et_sb[k2 % 2][:, c * BPC * P:(c * BPC + nblk) * P]
                src = bk(4 + n % 2)[:, 0:nblk * P]
                if by_dve:
                    nc.vector.tensor_copy(dst, src).then_inc(s_evD, 1)
                else:
                    nc.scalar.copy(dst, src).then_inc(s_evA, 1)

        def pairs(eng, body, lag):
            body(0, range(PAIR), True, False)
            with eng.Fori(1, NP) as p:
                body(p, range(PAIR), False, False)
            body(NP, range(lag), False, True)

        @block.sync
        def _(sp):
            for w, src in enumerate((wq_d, wk_d, wv_d)):
                sp.dma_start(wqkv[:, w], src.rearrange("(k p) d -> p k d", p=P)).then_inc(s_w, 16)
            for s in range(CPB):
                sp.dma_start(xc[s], x_t[:, s * TPC:(s + 1) * TPC, :]).then_inc(s_x[s], 16)
            sp.dma_start(router[:, :, :], router_d.rearrange("(k p) e -> p k e", p=P)).then_inc(s_w, 16)

            def store_parts(b, cc):
                c = CPB * b + cc
                for g in range(4):
                    sp.wait_ge(s_p3, 4 * c + g + 1)
                    ty, cg = divmod(g, KC)
                    sp.dma_start(qk_d[ty, :, ds(b * D + cg * P, P), cc * CT:(cc + 1) * CT]
                                 .rearrange("s r t -> r s t"), parts[g]).then_inc(s_st[g], 16)

            def load_next(b, cc):
                sp.wait_ge(s_xt, KC * (CPB * b + cc + 1))
                sp.dma_start(xc[cc], x_t[:, ds((CPB * (b + 1) + cc) * TPC, TPC), :]).then_inc(s_x[cc], 16)

            if NB > 1:
                with sp.Fori(0, NB - 1) as b:
                    for cc in range(CPB):
                        load_next(b, cc)
                        store_parts(b, cc)
            for cc in range(CPB):
                store_parts(NB - 1, cc)
            for g in range(4):
                sp.wait_ge(s_st[g], 16 * NB * CPB)

            Q_TERMS, K_TERMS = (0, 1, 2, 0, 1, 0), (0, 0, 0, 1, 1, 2)

            def load_head(h, s):
                for ty, (dst, terms) in enumerate(((qs[s], Q_TERMS), (ks[s], K_TERMS))):
                    for r, part in enumerate(terms):
                        sp.dma_start(dst[r * DH:(r + 1) * DH, :], qk_d[ty, part, ds(h * DH, DH), :])\
                          .then_inc(s_ld[s], 16)

            load_head(0, 0)
            load_head(1, 1)
            sp.wait_ge(s_ve, 2 * NB * CPB)
            sp.dma_start(x1[:, :, :], x_t).then_inc(s_xin, 16)
            wfc_v = wfc_d.rearrange("e (k p) f -> p (e k) f", p=P)
            wfc_s = wfc[:, :].rearrange("p (c f) -> p c f", f=FF)
            PIECES = 2 * E * KC
            HF = FF // 2

            def load_wfc(j):
                at = (slice(None), ds(j // 2, 1), ds((j % 2) * HF, HF))
                sp.dma_start(wfc_s[at], wfc_v[at]).then_inc(s_wfc, 16)

            for j in [0] + list(range(NP, PIECES)):
                load_wfc(j)
            with sp.Fori(1, NP) as p:
                load_wfc(p)
                for hl in range(2):
                    sp.wait_ge(s_S, PAIR * p + QT * hl - QT)
                    load_head(2 * p + hl, hl)

            sp.wait_ge(s_pv, NH * QT)
            for e in range(E):
                sp.dma_start(arena[:, e * WSTEP:(e + 1) * WSTEP].rearrange("p (c d) -> p c d", c=FC),
                             wproj_d[e].rearrange("(c p) d -> p c d", p=P)).then_inc(s_wp, 16)

            sp.wait_ge(s_sc, 16 * TT * TOPK)
            for s in range(2):
                sp.dma_start(xslot[s], xs_d[s * P:(s + 1) * P, :]).then_inc(s_xs[s], 16)

            def store_tile(t, s):
                sp.wait_ge(s_yo, t + 1)
                sp.dma_start(ys_d[ds(t * P, P), :], yslot[s]).then_inc(s_ys[s], 16)

            def load_tile(t, s):
                sp.wait_ge(s_mt, t - 1)
                sp.dma_start(xslot[s], xs_d[ds(t * P, P), :]).then_inc(s_xs[s], 16)

            NL = (NT - 3) // 2
            with sp.Fori(0, NL) as q:
                for s in range(2):
                    load_tile(2 * q + 2 + s, s)
                    store_tile(2 * q + s, s)
            for t in range(2 * NL + 2, NT):
                load_tile(t, t % 2)
            for t in range(2 * NL, NT):
                store_tile(t, t % 2)

            with sp.Fori(0, TT // 4) as g:
                for j in range(4):
                    sp.wait_ge(s_o, 4 * g + j + 1)
                    sp.dma_start(out_t[:, ds(4 * g + j, 1), :], ct[j][:, 1:2, :]).then_inc(s_out[j], 16)
            for j in range(4):
                sp.wait_ge(s_out[j], 16 * TT // 4)

        @block.gpsimd
        def _(pool):
            pool.memset(ident[:, :], 0.0).then_inc(s_const, 1)
            pool.memset(lower[:, :], 1.0).then_inc(s_const, 1)
            pool.memset(tle[:, :, :], 1.0).then_inc(s_const, 1)
            pool.memset(ones[:, :], 1.0).then_inc(s_const, 1)
            pool.memset(causal[:, :], 1.0).then_inc(s_const, 1)
            pool.memset(cst0[:, :], 0.0).then_inc(s_zero, 1)
            pool.memset(zero, 0.0).then_inc(s_zero, 1)
            pool.iota(iota_e[:, :], [[1, E]], base=0, channel_multiplier=0,
                      allow_small_or_imprecise_dtypes=True).then_inc(s_const, 1)
            pool.iota(thr[:, :], [[P, TT]], base=0, channel_multiplier=0,
                      allow_small_or_imprecise_dtypes=True).then_inc(s_const, 1)
            pool.iota(iota_t[:, :], [[1, NT]], base=0, channel_multiplier=0,
                      allow_small_or_imprecise_dtypes=True).then_inc(s_const, 1)
            pool.wait_ge(s_const, 8)
            pool.affine_select(out=ident[:, :], in_=ident[:, :], compare_op=ALU.not_equal, fill=1.0,
                               base=0, pattern=[[-1, P]], channel_multiplier=1).then_inc(s_ident, 1)
            pool.affine_select(out=lower[:, :], in_=lower[:, :], compare_op=ALU.is_gt, fill=0.0,
                               base=0, pattern=[[1, P]], channel_multiplier=-1).then_inc(s_const, 1)
            pool.affine_select(out=causal[:, :], in_=causal[:, :], compare_op=ALU.is_ge, fill=0.0, base=0,
                               pattern=[[-1, P]], channel_multiplier=1).then_inc(s_const, 1)
            pool.affine_select(out=tle[:, :, :], in_=tle[:, :, :], compare_op=ALU.is_ge, fill=0.0,
                               base=0, pattern=[[1, E], [-1, E]], channel_multiplier=0).then_inc(s_const, 1)
            def split(b, cc):
                for g in range(4):
                    n = 4 * (CPB * b + cc) + g
                    pool.wait_ge(s_p2, n + 1)
                    pool.tensor_tensor(parts[g][:, 2, :], resid[g % 2], parts[g][:, 1, :],
                                       ALU.subtract).then_inc(s_p3, 1)

            with pool.Fori(0, NB) as b:
                for cc in range(CPB):
                    split(b, cc)

            pool.wait_ge(s_zero, 2)
            for t in range(0, NT, 8):
                n = min(8, NT - t)
                pool.dma_start(xs_d[t * P:(t + n) * P, :].rearrange("(t p) d -> p t d", p=P),
                               zero.unsqueeze(1).to_broadcast([P, n, D])).then_inc(s_xsz, 16)

            def mask(p, ks_, first, tail):
                if tail:
                    return
                for k in ks_:
                    i = k % QT
                    pool.wait_ge(s_exp, PAIR * p + k + 1)
                    blk = e_sb[k % 4][:, i * P:(i + 1) * P]
                    pool.tensor_tensor(blk, blk, causal[:, :], ALU.mult).then_inc(s_mask, 1)

            pool.wait_ge(s_const, 11)
            mask(0, range(PAIR), True, False)
            with pool.Fori(1, NP) as p:
                mask(p, range(PAIR), False, False)

            pool.wait_ge(s_xin, 16)
            with pool.Fori(0, TT // TPC) as g:
                pool.wait_ge(s_y2, g + 1)
                pool.tensor_tensor(x1[:, ds(g * TPC, TPC), :], x1[:, ds(g * TPC, TPC), :],
                                   yx[:, ds(g * TPC, TPC), :], ALU.add).then_inc(s_add, 1)

            pool.wait_ge(s_pos, 1)
            pool.wait_ge(s_xsz, 16 * ((NT + 7) // 8))
            pool.wait_ge(s_x2, TT // TPC)
            for t in range(TT):
                for j in range(TOPK):
                    pool.indirect_dma_start(out=xs_d, out_offset=bass.IndirectOffsetOnAxis(ap=pos[:, j, t:t + 1], axis=0),
                                            in_=yx[:, t, :], in_offset=None).then_inc(s_sc, 16)

            for s in range(2):
                pool.wait_ge(s_ys[s], 16 * ((NT + 1 - s) // 2))
            for t in range(TT):
                if t >= NG:
                    pool.wait_ge(s_o, t - NG + 1)
                    pool.wait_ge(s_out[t % NG], 16 * (t // NG))
                for j in range(TOPK):
                    pool.indirect_dma_start(out=ct[t % NG][:, j, :], out_offset=None, in_=ys_d,
                                            in_offset=bass.IndirectOffsetOnAxis(ap=pos[:, j, t:t + 1], axis=0))\
                        .then_inc(s_g[t % NG], 16)

        @block.scalar
        def _(act):
            act.wait_ge(s_zero, 1)
            nc.scalar.activation(warm[:, 0:1], cst0[:, 0:1], ACT.Sqrt).then_inc(s_warm, 1)

            def project(b, cc):
                c = CPB * b + cc
                act.wait_ge(s_var, c + 1)
                nc.scalar.activation(std[:, cc, :], mv[:, cc, :, 1], ACT.Sqrt).then_inc(s_std, 1)
                act.wait_ge(s_xt, KC * c + 1)
                if not isinstance(c, int) or c >= 2:
                    act.wait_ge(s_v, 2 * (c - 1))
                nc.scalar.copy(xnT[cc][:, 0, :], bk(0)).then_inc(s_xta, 1)
                for g in range(4):
                    act.wait_ge(s_qk, 4 * c + g + 1)
                    if not isinstance(c, int) or c >= 1:
                        act.wait_ge(s_st[g], 16 * c)
                    nc.scalar.mul(parts[g][:, 0, :], bk(2 + g), Q_SCALE if g < KC else 1.0).then_inc(s_p1, 1)
                for j in range(2):
                    act.wait_ge(s_v, 2 * c + j + 1)
                    for t in range(2):
                        i = TPC * cc + 2 * j + t
                        dst = v_sb.rearrange("p (b h i d) -> p b h i d", b=NB, h=H, i=QT)[:, ds(b, 1), :, i, :]
                        ins = nc.scalar.copy(dst, bk(6 + j)[:, t * D:(t + 1) * D]
                                             .rearrange("p (b h d) -> p b h d", b=1, h=H))
                    ins.then_inc(s_ve, 1)

            for cc in range(CPB):
                project(0, cc)
            if NB > 1:
                with act.Fori(1, NB) as b:
                    for cc in range(CPB):
                        project(b, cc)
            act.wait_ge(s_warm, 1)
            nc.scalar.activation(warm[:, 1:2], cst0[:, 0:1], ACT.Exp).then_inc(s_warm, 1)

            def body(p, ks_, first, tail):
                for k in ks_:
                    copies(act, p, k, False, first, tail)
                    if not tail:
                        hl, i = unit(k)
                        act.wait_ge(s_max, PAIR * p + k + 1)
                        wait_pos(act, s_T, NC * 2 * p + count_T(k - 4))
                        if i == 0:
                            wait_pos(act, s_norm, 2 * p + hl - 1)
                        nc.scalar.activation(e_sb[k % 4], ps[:, 2 * (k % 2):2 * (k % 2) + 2, :], ACT.Exp,
                                             bias=negmax[:, hl, i:i + 1],
                                             accum_out=den[:, hl, i:i + 1]).then_inc(s_exp, 1)

            pairs(act, body, LAG_E)

            act.wait_ge(s_warm, 2)
            act.wait_ge(s_xsz, 16 * ((NT + 7) // 8))
            nc.scalar.activation(warm[:, 0:1], cst0[:, 0:1], ACT.Sqrt).then_inc(s_warm, 1)
            with act.Fori(0, TT // TPC) as g:
                for j in range(2):
                    act.wait_ge(s_var2, 2 * g + j + 1)
                    nc.scalar.activation(std[:, j, :], mv[:, j, :, 1], ACT.Sqrt).then_inc(s_std2, 1)
                for kc in range(KC):
                    act.wait_ge(s_x2t, KC * g + kc + 1)
                    nc.scalar.copy(x2T[:, kc, :], bk(kc)).then_inc(s_x2e, 1)
            act.wait_ge(s_warm, 3)
            act.wait_ge(s_d2, 1)
            nc.scalar.activation(gtmp[:, :], gtmp[:, :], ACT.Exp).then_inc(s_ex2, 1)
            nc.scalar.activation(warm[:, 1:2], cst0[:, 0:1], ACT.Gelu).then_inc(s_warm, 1)

            def mix(t):
                for hf in range(2):
                    act.wait_ge(s_fc, 2 * t + hf + 1)
                    wait_pos(act, s_ht, 2 * t)
                    nc.scalar.activation(hid[:, hf * 512:(hf + 1) * 512], bk(1 + hf), ACT.Gelu).then_inc(s_ge, 1)
                act.wait_ge(s_ht, 2 * t + 1)
                wait_pos(act, s_pr, t)
                nc.scalar.copy(hidT[:, 0:4, :], bk(3).rearrange("p (c t) -> p c t", c=4)).then_inc(s_hea, 1)

            mix(0)
            with act.Fori(1, NT) as t:
                mix(t)

            act.wait_ge(s_warm, 4)
            nc.scalar.activation(warm[:, 0:1], cst0[:, 0:1], ACT.Sqrt).then_inc(s_warm, 1)
            with act.Fori(0, TT) as t:
                act.wait_ge(s_var3, t + 1)
                nc.scalar.activation(std[:, 0, 0:1], mv[:, 0, 0, 1:2], ACT.Sqrt).then_inc(s_std3, 1)
            act.wait_ge(s_warm, 5)

        @block.tensor
        def _(pe):
            pe.wait_ge(s_ident, 1)
            pe.wait_ge(s_w, 64)

            def project(b, cc):
                c = CPB * b + cc
                pe.wait_ge(s_xn, c + 1)
                for kc in range(KC):
                    wait_pos(pe, (s_xta, s_xtd)[kc], c)
                    for t in range(TPC):
                        ins = nc.tensor.transpose(bk(kc)[:, t * P:(t + 1) * P], xc[cc][:, t, kc * P:(kc + 1) * P],
                                                  ident[:, :])
                    ins.then_inc(s_xt, 1)
                pe.wait_ge(s_xta, c + 1)
                pe.wait_ge(s_xtd, c + 1)
                for g in range(4):
                    wait_pos(pe, s_res, 4 * c + g - 3)
                    ty, cg = divmod(g, KC)
                    for kc in range(KC):
                        ins = nc.tensor.matmul(bk(2 + g), wqkv[:, ty, kc, cg * P:(cg + 1) * P], xnT[cc][:, kc, :],
                                               start=(kc == 0), stop=(kc == KC - 1))
                    ins.then_inc(s_qk, 1)
                for j in range(2):
                    wait_pos(pe, s_ve, 2 * c + j - 1)
                    for t in range(2):
                        for kc in range(KC):
                            ins = nc.tensor.matmul(bk(6 + j)[:, t * D:(t + 1) * D],
                                                   xnT[cc][:, kc, (2 * j + t) * P:(2 * j + t + 1) * P],
                                                   wqkv[:, 2, kc, :], start=(kc == 0), stop=(kc == KC - 1))
                    ins.then_inc(s_v, 1)

            for cc in range(CPB):
                project(0, cc)
            if NB > 1:
                with pe.Fori(1, NB) as b:
                    for cc in range(CPB):
                        project(b, cc)
            pe.wait_ge(s_res, 4 * NB * CPB)
            pe.wait_ge(s_ve, 2 * NB * CPB)

            def body(p, ks_, first, tail):
                for k in ks_:
                    if not tail:
                        hl, i = unit(k)
                        if i == 0:
                            pe.wait_ge(s_ld[hl], 16 * 2 * TERMS * (p + 1))
                        wait_pos(pe, s_exp, PAIR * p + k - 1)
                        for hf in range(2):
                            ins = nc.tensor.matmul(bk(2 * (k % 2) + hf), qs[hl][0:SROWS, i * P:(i + 1) * P],
                                                   ks[hl][0:SROWS, hf * 512:(hf + 1) * 512], start=True, stop=True)
                        ins.then_inc(s_S, 1)
                    k2 = k - LAG_T
                    if not (first and k2 < 0) and not (tail and k2 >= 0):
                        hl, i = unit(k2)
                        pe.wait_ge(s_mask, PAIR * p + k2 + 1)
                        for (_, c, nblk, n, n_d, n_a) in of_unit[i]:
                            copied(pe, p, hl, n - 2)
                            b_ = bk(4 + n % 2)
                            for j in range(nblk):
                                kb = BPC * c + j
                                ins = nc.tensor.transpose(b_[:, j * P:(j + 1) * P],
                                                          e_sb[k2 % 4][:, kb * P:(kb + 1) * P], ident[:, :])
                            ins.then_inc(s_T, 1)
                    k3 = k - LAG_V
                    if not (first and k3 < 0) and not (tail and k3 >= 0):
                        hl, i = unit(k3)
                        h = 2 * p + hl
                        for ch in of_unit[i]:
                            copied(pe, p, hl, ch[3])
                        if i == 0:
                            wait_pos(pe, s_norm, 2 * p + hl - 1)
                        for kb in range(i + 1):
                            ins = nc.tensor.matmul(bk(6 + hl % 2)[:, i * DH:(i + 1) * DH],
                                                   et_sb[k3 % 2][:, kb * P:(kb + 1) * P],
                                                   v_sb[:, ds(h * QT * DH + kb * DH, DH)],
                                                   start=(kb == 0), stop=(kb == i))
                        ins.then_inc(s_pv, 1)

            pairs(pe, body, LAG_V)

            pe.wait_ge(s_evA, NA * NH)
            pe.wait_ge(s_exp, QT * NH)
            pe.wait_ge(s_norm, NH)

            def route(g):
                pe.wait_ge(s_x2, g + 1)
                for kc in range(KC):
                    wait_pos(pe, s_x2e, KC * g + kc - 1)
                    for t in range(TPC):
                        ins = nc.tensor.transpose(bk(kc)[:, t * P:(t + 1) * P],
                                                  yx[:, g * TPC + t, kc * P:(kc + 1) * P], ident[:, :])
                    ins.then_inc(s_x2t, 1)
                pe.wait_ge(s_x2e, KC * (g + 1))
                for t in range(TPC):
                    for kc in range(KC):
                        ins = nc.tensor.matmul(bk(2)[:, (g * TPC + t) * E:(g * TPC + t + 1) * E],
                                               x2T[:, kc, t * P:(t + 1) * P], router[:, kc, :],
                                               start=(kc == 0), stop=(kc == KC - 1))
                ins.then_inc(s_lg, 1)

            for g in range(TT // TPC):
                route(g)

            pe.wait_ge(s_oh, 1)
            pe.wait_ge(s_const, 11)
            rank = bk(3)[:, 0:(TT + 1) * E].rearrange("p (t e) -> p t e", e=E)
            nc.tensor.matmul(rank[:, 0:TT, :], lower[:, :], oh_bf[:, :, :], start=True, stop=False,
                             skip_group_check=True)
            for t in range(TT):
                n = TT - t
                ins = nc.tensor.matmul(rank[:, t + 1:TT + 1, :], ones[:, :],
                                       oh_bf[:, t, :].unsqueeze(1).to_broadcast([P, n, E]),
                                       start=False, stop=(t == TT - 1), skip_group_check=True)
            ins.then_inc(s_rank, 1)

            pe.wait_ge(s_tab, 1)
            pe.wait_ge(s_wfc, 16 * 2 * E * KC)

            def transpose_x(t, s):
                pe.wait_ge(s_xs[s], 16 * (t // 2 + 1) if isinstance(t, int) else t * 8 + 8 * (2 - s))
                wait_pos(pe, s_me, t)
                for kc in range(KC):
                    ins = nc.tensor.transpose(bk(0)[:, kc * P:(kc + 1) * P], xslot[s][:, kc * P:(kc + 1) * P],
                                              ident[:, :])
                ins.then_inc(s_mt, 1)

            def first_product(t, off):
                pe.wait_ge(s_me, t + 1)
                for hf in range(2):
                    wait_pos(pe, s_ge, 2 * t + hf - 1)
                    for kc in range(KC):
                        ins = nc.tensor.matmul(bk(1 + hf), xsT[:, kc, :],
                                               wfc[:, ds(off + (kc * FF + hf * 512), 512)],
                                               start=(kc == 0), stop=(kc == KC - 1))
                    ins.then_inc(s_fc, 1)

            def transpose_h(t):
                for hf in range(2):
                    pe.wait_ge(s_ge, 2 * t + hf + 1)
                    wait_pos(pe, (s_hea, s_hed)[hf], t)
                    for c in range(4):
                        ins = nc.tensor.transpose(bk(3 + hf)[:, c * P:(c + 1) * P],
                                                  hid[:, (4 * hf + c) * P:(4 * hf + c + 1) * P], ident[:, :])
                    ins.then_inc(s_ht, 1)

            def second_product(t, s, off):
                wait_pos(pe, s_yo, t - 1)
                pe.wait_ge(s_hea, t + 1)
                for c in range(FC):
                    if c == FC // 2:
                        pe.wait_ge(s_hed, t + 1)
                    ins = nc.tensor.matmul(bk(5 + s)[:, 0:D], hidT[:, c, :], arena[:, ds(off + c * D, D)],
                                           start=(c == 0), stop=(c == FC - 1))
                ins.then_inc(s_pr, 1)

            def expert(t):
                return pe.value_load(tab[0:1, ds(t, 1)], min_val=0, max_val=(E - 1) * WSTEP)

            def step(t, s, first=False, last=False):
                if not first:
                    transpose_h(t - 1)
                if not last:
                    first_product(t, expert(t))
                    if not (isinstance(t, int) and t == NT - 1):
                        transpose_x(t + 1, 1 - s)
                if not first:
                    second_product(t - 1, 1 - s, expert(t - 1))

            transpose_x(0, 0)
            step(0, 0, first=True)
            pe.wait_ge(s_wp, 16 * E)
            step(1, 1)
            step(2, 0)
            NL2 = (NT - 4) // 2
            with pe.Fori(0, NL2) as q:
                step(2 * q + 3, 1)
                step(2 * q + 4, 0)
            for t in range(2 * NL2 + 3, NT):
                step(t, t % 2)
            step(NT, NT % 2, last=True)

        @block.vector
        def _(dve):
            def ln_stats(src, s, n, s_chain, chain0, s_out_):
                for t in range(n):
                    nc.vector.bn_stats(stats[:, s, t, :], src[t]).then_inc(s_chain, 1)
                dve.wait_ge(s_chain, chain0 + n)
                nc.vector.memset(pause[:, :], 0.0)
                for t in range(n):
                    nc.vector.bn_aggr(mv[:, s, t, :], stats[:, s, t, :]).then_inc(s_chain, 1)
                dve.wait_ge(s_chain, chain0 + 2 * n)
                nc.vector.tensor_scalar(mv[:, s, 0:n, 1], mv[:, s, 0:n, 1], EPS, None, ALU.add).then_inc(s_out_, 1)

            def ln_apply(dst, src, s, n, s_chain, chain1):
                nc.vector.reciprocal(rstd[:, s, 0:n], std[:, s, 0:n]).then_inc(s_chain, 1)
                dve.wait_ge(s_chain, chain1)
                for t in range(n):
                    ins = nc.vector.tensor_scalar(dst[t], src[t], mv[:, s, t, 0:1], rstd[:, s, t:t + 1],
                                                  ALU.subtract, ALU.mult)
                return ins

            CH = 2 * TPC + 1

            def project(b, cc):
                c = CPB * b + cc
                dve.wait_ge(s_x[cc], 16 * (b + 1))
                rows = [xc[cc][:, t, :] for t in range(TPC)]
                ln_stats(rows, cc, TPC, s_bn, CH * c, s_var)
                dve.wait_ge(s_std, c + 1)
                ln_apply(rows, rows, cc, TPC, s_bn, CH * (c + 1)).then_inc(s_xn, 1)
                dve.wait_ge(s_xt, KC * (c + 1))
                if not isinstance(c, int) or c >= 2:
                    dve.wait_ge(s_v, 2 * (c - 1))
                nc.vector.tensor_copy(xnT[cc][:, 1, :], bk(1)).then_inc(s_xtd, 1)
                for g in range(4):
                    dve.wait_ge(s_p1, 4 * c + g + 1)
                    wait_pos(dve, s_p3, 4 * c + g - 1)
                    nc.vector.scalar_tensor_tensor(out=resid[g % 2], in0=bk(2 + g),
                                                   scalar=Q_SCALE if g < KC else 1.0, in1=parts[g][:, 0, :],
                                                   op0=ALU.mult, op1=ALU.subtract).then_inc(s_res, 1)
                    dve.wait_ge(s_res, 4 * c + g + 1)
                    if not isinstance(c, int) or c >= 1:
                        dve.wait_ge(s_st[g], 16 * c)
                    nc.vector.tensor_copy(parts[g][:, 1, :], resid[g % 2]).then_inc(s_p2, 1)

            for cc in range(CPB):
                project(0, cc)
            if NB > 1:
                with dve.Fori(1, NB) as b:
                    for cc in range(CPB):
                        project(b, cc)

            def body(p, ks_, first, tail):
                for k in ks_:
                    if not tail:
                        hl, i = unit(k)
                        dve.wait_ge(s_S, PAIR * p + k + 1)
                        nc.vector.tensor_reduce(negmax[:, hl, i:i + 1], ps[:, 2 * (k % 2):2 * (k % 2) + 2, :],
                                                AX.XY, ALU.max, negate=True).then_inc(s_max, 1)
                    copies(dve, p, k, True, first, tail)
                    k4 = k - LAG_N
                    if k4 % QT == QT - 1 and not (first and k4 < 0) and not (tail and k4 >= 0):
                        hl, _ = unit(k4)
                        n = 2 * p + hl + 1
                        h = 2 * p + hl
                        dve.wait_ge(s_pv, PAIR * p + k4 + 1)
                        nc.vector.reciprocal(rden[:, hl % 2, :], den[:, hl % 2, :]).then_inc(s_rc, 1)
                        dve.wait_ge(s_rc, n)
                        hh, bb = h % H, h // H
                        dst = yx[:, ds(bb * QT, QT), ds(hh * DH, DH)]
                        nc.vector.tensor_tensor(dst, bk(6 + hl % 2)[:, 0:QT * DH].rearrange("p (i d) -> p i d", d=DH),
                                                rden[:, hl % 2, :].unsqueeze(2).to_broadcast([P, QT, DH]),
                                                ALU.mult).then_inc(s_norm, 1)

            pairs(dve, body, LAG_N + 1)
            dve.wait_ge(s_norm, NH)

            CH2 = 2 * CH
            with dve.Fori(0, TT // TPC) as g:
                yr = [yx[:, ds(g * TPC + t, 1), :] for t in range(TPC)]
                xr = [x1[:, ds(g * TPC + t, 1), :] for t in range(TPC)]
                ln_stats(yr, 0, TPC, s_bn2, CH2 * g, s_var2)
                dve.wait_ge(s_std2, 2 * g + 1)
                ln_apply(yr, yr, 0, TPC, s_bn2, CH2 * g + CH).then_inc(s_y2, 1)
                dve.wait_ge(s_add, g + 1)
                ln_stats(xr, 1, TPC, s_bn2, CH2 * g + CH, s_var2)
                dve.wait_ge(s_std2, 2 * g + 2)
                ln_apply(yr, xr, 1, TPC, s_bn2, CH2 * (g + 1)).then_inc(s_x2, 1)

            n_r = [0]

            def link(ins):
                n_r[0] += 1
                ins.then_inc(s_r, 1)
                dve.wait_ge(s_r, n_r[0])

            dve.wait_ge(s_lg, TT // TPC)
            link(nc.vector.tensor_copy(lg[:, :, :].rearrange("p t e -> p (t e)"), bk(2)[:, 0:TT * E]))
            for t in range(TT):
                ins = nc.vector.max(top[:, t, :], lg[:, t, :])
            link(ins)
            for t in range(TT):
                ins = nc.vector.max_index(topi[:, t, :], top[:, t, :], lg[:, t, :])
            link(ins)
            nc.vector.tensor_tensor(gtmp[:, :], top[:, :, 1], top[:, :, 0], ALU.subtract).then_inc(s_d2, 1)
            for j in range(TOPK):
                ins = nc.vector.tensor_copy(choice[:, j, :], topi[:, :, j])
            link(ins)
            dve.wait_ge(s_const, 11)
            for j in range(TOPK):
                ins = nc.vector.tensor_tensor(oh[:, j, :, :], choice[:, j, :].unsqueeze(2).to_broadcast([P, TT, E]),
                                              iota_e[:, :].unsqueeze(1).to_broadcast([P, TT, E]), ALU.is_equal)
            link(ins)
            nc.vector.tensor_tensor(oh_bf[:, :, :], oh[:, 0], oh[:, 1], ALU.add).then_inc(s_oh, 1)
            dve.wait_ge(s_ex2, 1)
            link(nc.vector.tensor_scalar(gate[:, 1, :], gtmp[:, :], 1.0, None, ALU.add))
            link(nc.vector.reciprocal(gate[:, 0, :], gate[:, 1, :]))
            link(nc.vector.tensor_tensor(gate[:, 1, :], gate[:, 0, :], gtmp[:, :], ALU.mult))
            dve.wait_ge(s_rank, 1)
            rank = bk(3)[:, 0:(TT + 1) * E].rearrange("p (t e) -> p t e", e=E)
            link(nc.vector.tensor_copy(cnt[:, :], rank[:, TT, :]))
            link(nc.vector.tensor_tensor(tmp_t[:, :, :], cnt[:, :].unsqueeze(2).to_broadcast([P, E, TT]),
                                         thr[:, :].unsqueeze(1).to_broadcast([P, E, TT]), ALU.is_gt))
            link(nc.vector.tensor_reduce(ntile[:, :], tmp_t[:, :, :], AX.X, ALU.add))
            link(nc.vector.tensor_tensor(tmp_e[:, :, :], tle[:, :, :], ntile[:, :].unsqueeze(1).to_broadcast([P, E, E]),
                                         ALU.mult))
            link(nc.vector.tensor_reduce(endt[:, :], tmp_e[:, :, :], AX.X, ALU.add))
            link(nc.vector.tensor_tensor(base[:, :], endt[:, :], ntile[:, :], ALU.subtract))
            link(nc.vector.tensor_scalar(base[:, :], base[:, :], float(P), None, ALU.mult))
            link(nc.vector.tensor_tensor(tmp[:, :, :], rank[:, 0:TT, :], base[:, :].unsqueeze(1).to_broadcast([P, TT, E]),
                                         ALU.add))
            for j in range(TOPK):
                ins = nc.vector.tensor_tensor(oh[:, j], oh[:, j], tmp[:, :, :], ALU.mult)
            link(ins)
            for j in range(TOPK):
                ins = nc.vector.tensor_reduce(posf[:, j, :], oh[:, j], AX.X, ALU.add)
            link(ins)
            nc.vector.tensor_copy(pos[:, :, :], posf[:, :, :]).then_inc(s_pos, 1)
            link(nc.vector.tensor_tensor(tmp_n[:, :, :], endt[0:1, :].unsqueeze(1).to_broadcast([1, NT, E]),
                                         iota_t[:, :].unsqueeze(2).to_broadcast([1, NT, E]), ALU.is_le))
            link(nc.vector.tensor_reduce(tabf[:, :], tmp_n[:, :, :], AX.X, ALU.add))
            link(nc.vector.tensor_scalar(tabf[:, :], tabf[:, :], float(E - 1), float(WSTEP), ALU.min, ALU.mult))
            nc.vector.tensor_copy(tab[:, :], tabf[:, :]).then_inc(s_tab, 1)

            def copy_x(t):
                dve.wait_ge(s_mt, t + 1)
                wait_pos(dve, s_fc, 2 * t)
                nc.vector.tensor_copy(xsT[:, :, :], bk(0)[:, 0:KC * P].rearrange("p (k t) -> p k t", k=KC))\
                  .then_inc(s_me, 1)

            def copy_h(t):
                dve.wait_ge(s_ht, 2 * t + 2)
                wait_pos(dve, s_pr, t)
                nc.vector.tensor_copy(hidT[:, 4:8, :], bk(4).rearrange("p (c t) -> p c t", c=4)).then_inc(s_hed, 1)

            def copy_y(t, s):
                dve.wait_ge(s_pr, t + 1)
                if not isinstance(t, int) or t >= 2:
                    dve.wait_ge(s_ys[s], 16 * (t // 2) if isinstance(t, int) else 8 * t - 8 * s)
                nc.vector.tensor_copy(yslot[s], bk(5 + s)[:, 0:D]).then_inc(s_yo, 1)

            def mix(t, s):
                if not isinstance(t, int) or t >= 1:
                    copy_h(t - 1)
                if not isinstance(t, int) or t < NT - 1:
                    copy_x(t + 1)
                if not isinstance(t, int) or t >= 1:
                    copy_y(t - 1, 1 - s)

            copy_x(0)
            mix(0, 0)
            mix(1, 1)
            mix(2, 0)
            NL3 = (NT - 4) // 2
            with dve.Fori(0, NL3) as q:
                mix(2 * q + 3, 1)
                mix(2 * q + 4, 0)
            for t in range(2 * NL3 + 3, NT + 1):
                mix(t, t % 2)

            CC = 6
            with dve.Fori(0, TT // NG) as g:
                for j in range(NG):
                    t = NG * g + j
                    dve.wait_ge(s_g[j], 32 * (g + 1))
                    y0, y1 = ct[j][:, 0:1, :], ct[j][:, 1:2, :]
                    nc.vector.tensor_scalar(y0, y0, gate[:, 0, ds(t, 1)], None, ALU.mult).then_inc(s_cc, 1)
                    dve.wait_ge(s_cc, CC * t + 1)
                    nc.vector.scalar_tensor_tensor(out=y0, in0=y1, scalar=gate[:, 1, ds(t, 1)], in1=y0,
                                                   op0=ALU.mult, op1=ALU.add).then_inc(s_cc, 1)
                    dve.wait_ge(s_cc, CC * t + 2)
                    ln_stats([y0], 0, 1, s_cc, CC * t + 2, s_var3)
                    dve.wait_ge(s_std3, t + 1)
                    ln_apply([y0], [y0], 0, 1, s_cc, CC * t + 5).then_inc(s_cc, 1)
                    dve.wait_ge(s_cc, CC * t + 6)
                    nc.vector.tensor_tensor(y1, y0, x1[:, ds(t, 1), :], ALU.add).then_inc(s_o, 1)


_INS = ['L0_attn_content', 'L0_attn_Wq', 'L0_attn_Wk', 'L0_attn_Wv', 'L0_ffn_router_w', 'L0_ffn_w_fc', 'L0_ffn_w_proj']


def kernel(**inputs):
    import numpy as _np
    import concourse.bacc as _bacc
    from concourse import mybir as _mybir
    from concourse.bass_utils import run_bass_kernel_spmd as _run

    nc = _bacc.Bacc("TRN2", target_bir_lowering=False, num_devices=1)
    arrays, args = {}, []
    for name in _INS:
        a = _np.ascontiguousarray(inputs[name])
        arrays[f"in_{name}"] = a
        args.append(nc.dram_tensor(f"in_{name}", a.shape, _mybir.dt.from_np(a.dtype), kind="ExternalInput").ap())
    shape = inputs[_INS[0]].shape
    args.append(nc.dram_tensor("out_0", shape, _mybir.dt.float32, kind="ExternalOutput").ap())
    sandwich(nc, *args)
    r = _run(nc, [arrays], core_ids=[0])
    return r.results[0]["out_0"]
```

```python
import concourse.bass as bass
from concourse import mybir
from contextlib import ExitStack


def sandwich(nc, x_d, wq_d, wk_d, wv_d, router_d, wfc_d, wproj_d, out_d):
    F32, BF16, I32, U32 = mybir.dt.float32, mybir.dt.bfloat16, mybir.dt.int32, mybir.dt.uint32
    ACT = mybir.ActivationFunctionType
    ALU = mybir.AluOpType
    AX = mybir.AxisListType
    ds = bass.ds

    P = 128
    NB, N, D = x_d.shape
    H, DH = 16, D // 16
    KC = D // P
    QT = N // P
    NH = NB * H
    TT = NB * QT
    E, _, FF = wfc_d.shape
    FC = FF // P
    TOPK = 2
    NT = TT * TOPK + E - 1
    CT = 512
    TPC = CT // P
    CPB = N // CT
    TERMS = 6
    SROWS = TERMS * DH
    Q_SCALE = DH ** -0.5
    EPS = 1e-5
    WSTEP = KC * FF
    assert WSTEP == FC * D and CPB == 2 and N == 1024

    qk_d = nc.dram_tensor("qk_parts", [2, 3, NB * D, N], BF16, kind="Internal").ap()
    xs_d = nc.dram_tensor("expert_in", [NT * P, D], F32, kind="Internal").ap()
    ys_d = nc.dram_tensor("expert_out", [NT * P, D], F32, kind="Internal").ap()

    x_t = x_d.rearrange("b (i p) d -> p (b i) d", p=P)
    out_t = out_d.rearrange("b (i p) d -> p (b i) d", p=P)

    ctx = ExitStack()
    with ctx:
        def sb(name, shape, dt=F32):
            return ctx.enter_context(nc.sbuf_tensor(name, shape, dt))

        def sem(name):
            return ctx.enter_context(nc.semaphore(name))

        wfc = sb("wfc", [P, E * WSTEP])
        arena = sb("arena", [P, E * WSTEP])
        yx = sb("yx", [P, TT, D])
        x1 = sb("x1", [P, TT, D])

        KB = 256
        v_sb = arena[:, 0:NH * QT * DH]
        a0 = NH * QT * DH
        qs = [arena[:, a0 + s * 2 * KB:a0 + (s + 1) * 2 * KB].bitcast(BF16) for s in range(4)]
        a0 += 8 * KB
        ks = [arena[:, a0 + s * 2 * KB:a0 + (s + 1) * 2 * KB].bitcast(BF16) for s in range(4)]
        a0 += 8 * KB
        NET = 6
        et_sb = [arena[:, a0 + s * 512:a0 + (s + 1) * 512] for s in range(NET)]
        a0 += NET * 512
        VW = DH + 1
        vh = [arena[:, a0 + s * QT * VW:a0 + (s + 1) * QT * VW].rearrange("p (i d) -> p i d", d=VW) for s in range(2)]
        a0 += 2 * QT * VW
        assert a0 <= E * WSTEP

        yx_f = yx[:, :, :].rearrange("p t d -> p (t d)")
        x1_f = x1[:, :, :].rearrange("p t d -> p (t d)")
        if NB == 4:
            pa, pb = yx_f, x1_f
        else:
            pa = sb("pa", [P, 32 * KB])[:, :]
            pb = sb("pb", [P, 16 * KB])[:, :]
        xc = [pa[:, s * TPC * D:(s + 1) * TPC * D].rearrange("p (t d) -> p t d", d=D) for s in range(2)]
        o = 2 * TPC * D
        xnT = [pa[:, o + s * KC * CT:o + (s + 1) * KC * CT].rearrange("p (k t) -> p k t", k=KC) for s in range(2)]
        o += 2 * KC * CT
        wqkv = pa[:, o:o + 3 * KC * D].rearrange("p (w k d) -> p w k d", w=3, k=KC)
        parts = [pb[:, g * 3 * KB:(g + 1) * 3 * KB].bitcast(BF16).rearrange("p (s t) -> p s t", s=3)
                 for g in range(4)]
        o = 12 * KB
        resid = [pb[:, o + s * CT:o + (s + 1) * CT] for s in range(2)]

        ident = sb("ident", [P, P])
        stats = sb("stats", [P, 2, TPC, 6])
        mv = sb("mv", [P, 2, TPC, 2])
        std = sb("std", [P, 2, TPC])
        rstd = sb("rstd", [P, 2, TPC])
        negmax = sb("negmax", [P, 2, QT])
        den = sb("den", [P, 4, QT])
        den_u = sb("den_u", [P, 4, QT])
        den_t = sb("den_t", [P, QT, 4])
        rden = sb("rden", [P, QT, 4])
        mparts = sb("mparts", [P, 2, 3, QT], BF16)
        mres = sb("mres", [P, 2, QT])
        zero8 = sb("zero8", [P, QT])
        mT = sb("mT", [P, P], BF16)
        dmask = sb("dmask", [P, QT])
        identb = sb("identb", [P, P], BF16)
        warm = sb("warm", [P, 2])
        pause = sb("pause", [P, 1])
        causal = sb("causal", [P, P])
        cst0 = sb("cst0", [P, 1])
        router = sb("router", [P, KC, E])
        rt = sb("rt", [P, 1280])
        po_sb = rt[:, 0:N]
        lg = rt[:, 0:TT * E].rearrange("p (t e) -> p t e", e=E)
        top = rt[:, 256:256 + TT * 8].rearrange("p (t e) -> p t e", e=8)
        topi = rt[:, 512:512 + TT * 8].bitcast(U32).rearrange("p (t e) -> p t e", e=8)
        oh = rt[:, 768:768 + TOPK * TT * E].rearrange("p (j t e) -> p j t e", j=TOPK, e=E)
        choice = sb("choice", [P, TOPK, TT])
        oh_bf = sb("oh_bf", [P, TT, E], BF16)
        gate = sb("gate", [P, TOPK, TT])
        gtmp = sb("gtmp", [P, TT])
        iota_e = sb("iota_e", [P, E])
        lower = sb("lower", [P, P], BF16)
        ones = sb("ones", [P, P], BF16)
        thr = sb("thr", [P, TT])
        cnt = sb("cnt", [P, E])
        ntile = sb("ntile", [P, E])
        tle = sb("tle", [P, E, E])
        endt = sb("endt", [P, E])
        base = sb("base", [P, E])
        posf = sb("posf", [P, TOPK, TT])
        pos = sb("pos", [P, TOPK, TT], I32)
        iota_t = sb("iota_t", [1, NT])
        tabf = sb("tabf", [1, NT])
        tab = sb("tab", [1, NT], I32)
        x2T = sb("x2T", [P, KC, CT])
        zero = x2T[:, 0, 0:D]
        tmp_e = sb("tmp_e", [P, E, E])
        x2T_f = x2T[:, :, :].rearrange("p k t -> p (k t)")
        tmp = x2T_f[:, 0:TT * E].rearrange("p (t e) -> p t e", e=E)
        tmp_t = x2T_f[:, TT * E:2 * TT * E].rearrange("p (e t) -> p e t", e=E)
        tmp_n = x2T_f[0:1, 0:NT * E].rearrange("p (t e) -> p t e", e=E)

        NG = 8
        ym = yx_f if NB == 4 else pa
        o = 0

        def piece(n):
            nonlocal o
            o += n
            return ym[:, o - n:o]

        xslot = [piece(D) for _ in range(2)]
        yslot = [piece(D) for _ in range(2)]
        hid = piece(FF)
        hidT = piece(FF).rearrange("p (c t) -> p c t", c=FC)
        xsT = piece(KC * P).rearrange("p (k t) -> p k t", k=KC)
        ct = [piece(2 * D).rearrange("p (j d) -> p j d", j=2) for _ in range(NG)]

        ps = ctx.enter_context(nc.psum_tensor("ps", [P, 8, 512], F32))

        def bk(i):
            return ps[:, i, :]

        s_w = sem("s_w")
        s_ident = sem("s_ident")
        s_const = sem("s_const")
        s_x = [sem("s_x0"), sem("s_x1")]
        s_bn = sem("s_bn")
        s_var = sem("s_var")
        s_std = sem("s_std")
        s_xn = sem("s_xn")
        s_xt = sem("s_xt")
        s_xta = sem("s_xta")
        s_xtd = sem("s_xtd")
        s_qk = sem("s_qk")
        s_p1 = sem("s_p1")
        s_res = sem("s_res")
        s_p2 = sem("s_p2")
        s_p3 = sem("s_p3")
        s_st = [sem(f"s_st{g}") for g in range(4)]
        s_v = sem("s_v")
        s_ve = sem("s_ve")
        s_wfc = sem("s_wfc")
        s_ld = [sem(f"s_ld{i}") for i in range(4)]
        s_S = sem("s_S")
        s_max = sem("s_max")
        s_exp = sem("s_exp")
        s_denc = sem("s_denc")
        s_sp = sem("s_sp")
        s_mtp = sem("s_mtp")
        s_mtc = sem("s_mtc")
        s_ex = sem("s_ex")
        s_vc = sem("s_vc")
        s_ST = sem("s_ST")
        s_expB = sem("s_expB")
        s_mask = sem("s_mask")
        s_pv = sem("s_pv")
        s_poz = sem("s_poz")
        s_poc = sem("s_poc")
        s_T4 = sem("s_T4")
        s_oc = sem("s_oc")
        s_nc = sem("s_nc")
        s_norm = sem("s_norm")
        s_zero = sem("s_zero")
        s_xsz = sem("s_xsz")
        s_xin = sem("s_xin")
        s_wp = sem("s_wp")
        s_bny = sem("s_bny")
        s_vary = sem("s_vary")
        s_stdy = sem("s_stdy")
        s_bnx = sem("s_bnx")
        s_varx = sem("s_varx")
        s_stdx = sem("s_stdx")
        s_y2 = sem("s_y2")
        s_add = sem("s_add")
        s_x2 = sem("s_x2")
        s_x2t = sem("s_x2t")
        s_x2e = sem("s_x2e")
        s_lg = sem("s_lg")
        s_r = sem("s_r")
        s_d2 = sem("s_d2")
        s_ex2 = sem("s_ex2")
        s_oh = sem("s_oh")
        s_rank = sem("s_rank")
        s_pos = sem("s_pos")
        s_tab = sem("s_tab")
        s_sc = sem("s_sc")
        s_xs = [sem("s_xs0"), sem("s_xs1")]
        s_mt = sem("s_mt")
        s_me = sem("s_me")
        s_fc = sem("s_fc")
        s_ge = sem("s_ge")
        s_ht = sem("s_ht")
        s_hea = sem("s_hea")
        s_hed = sem("s_hed")
        s_pr = sem("s_pr")
        s_yo = sem("s_yo")
        s_ys = [sem("s_ys0"), sem("s_ys1")]
        s_g = [sem(f"s_g{i}") for i in range(NG)]
        s_cf = sem("s_cf")
        s_cb = sem("s_cb")
        s_var3 = sem("s_var3")
        s_std3 = sem("s_std3")
        s_o = sem("s_o")
        s_out = [sem(f"s_out{i}") for i in range(NG)]
        s_warm = sem("s_warm")

        block = ctx.enter_context(nc.Block())

        U = 4 * QT
        NGR = NH // 4
        LAG_M, LAG_E, LAG_B, LAG_P = 9, 10, 12, 14
        STEP_C, STEP_T, STEP_N, TAIL = (10, 13), (12, 16), (12, 16), 19
        STEP_D = 2 * QT + 2
        MROW = 96
        MR = 3 * QT
        assert SROWS == MROW and N == 1024

        chunks = []
        for i in range(QT):
            for q0, q1 in ((i * P, 512), (max(i * P, 512), N)):
                if q0 < q1:
                    chunks.append((i, q0, q1 - q0, len(chunks)))
        NC = len(chunks)
        of_tile = {i: [ch for ch in chunks if ch[0] == i] for i in range(QT)}
        assert NC % NET == 0

        events = []
        for k in range(U):
            if k in STEP_T:
                events.append(("t", k, -4, STEP_T.index(k)))
            if (k - LAG_M) % QT == 0:
                events.append(("m", k, (k - LAG_M) // QT, 0))
            for ch in of_tile[(k - LAG_B) % QT]:
                events.append(("s", k, (k - LAG_B) // QT, ch[3]))
        assert len(events) % 2 == 0
        at_event = {ev: n for n, ev in enumerate(events)}

        def ebank(kind, k, hl, c):
            return 4 + at_event[(kind, k, hl, c)] % 2

        def free_bank(pe, p, first, tail, ev):
            n = at_event[ev] - 2
            while True:
                back, m = (1, n + len(events)) if n < 0 else (0, n)
                kind, _, hl, c = events[m]
                if first and back:
                    return
                if not back and not live(hl, first, tail):
                    n -= 2
                    continue
                h = 4 * p + hl - 4 * back
                if kind == "m":
                    pe.wait_ge(s_mtc, h + 1)
                elif kind == "s":
                    pe.wait_ge(s_expB, NC * h + c + 1)
                else:
                    pe.wait_ge(s_oc, 2 * (p - back - 1) + c + 1)
                return

        def live(u, first, tail):
            return not (first and u < 0) and not (tail and u >= 0)

        def wait_pos(eng, s, v):
            if isinstance(v, int) and v <= 0:
                return
            eng.wait_ge(s, v)

        def groups(eng, body):
            body(0, range(U), True, False)
            with eng.Fori(1, NGR) as p:
                body(p, range(U), False, False)
            body(NGR, range(TAIL), False, True)

        @block.sync
        def _(sp):
            for w, src in enumerate((wq_d, wk_d, wv_d)):
                sp.dma_start(wqkv[:, w], src.rearrange("(k p) d -> p k d", p=P)).then_inc(s_w, 16)
            for s in range(CPB):
                sp.dma_start(xc[s], x_t[:, s * TPC:(s + 1) * TPC, :]).then_inc(s_x[s], 16)
            sp.dma_start(router[:, :, :], router_d.rearrange("(k p) e -> p k e", p=P)).then_inc(s_w, 16)

            def store_parts(b, cc):
                c = CPB * b + cc
                for g in range(4):
                    sp.wait_ge(s_p3, 4 * c + g + 1)
                    ty, cg = divmod(g, KC)
                    sp.dma_start(qk_d[ty, :, ds(b * D + cg * P, P), cc * CT:(cc + 1) * CT]
                                 .rearrange("s r t -> r s t"), parts[g]).then_inc(s_st[g], 16)

            def load_next(b, cc):
                sp.wait_ge(s_xt, KC * (CPB * b + cc + 1))
                sp.dma_start(xc[cc], x_t[:, ds((CPB * (b + 1) + cc) * TPC, TPC), :]).then_inc(s_x[cc], 16)

            if NB > 1:
                with sp.Fori(0, NB - 1) as b:
                    for cc in range(CPB):
                        load_next(b, cc)
                        store_parts(b, cc)
            Q_TERMS, K_TERMS = (0, 1, 2, 0, 1, 0), (0, 0, 0, 1, 1, 2)

            def load_head(h, s):
                for ty, (dst, terms) in enumerate(((qs[s], Q_TERMS), (ks[s], K_TERMS))):
                    for r, part in enumerate(terms):
                        sp.dma_start(dst[r * DH:(r + 1) * DH, :], qk_d[ty, part, ds(h * DH, DH), :])\
                          .then_inc(s_ld[s], 16)

            def first_heads():
                sp.wait_ge(s_const, 17)
                for g in range(4):
                    sp.wait_ge(s_st[g], 16 * CPB)
                for hl in range(4):
                    load_head(hl, hl)

            if NB > 1:
                first_heads()
            for cc in range(CPB):
                store_parts(NB - 1, cc)
            if NB == 1:
                first_heads()
            for g in range(4):
                sp.wait_ge(s_st[g], 16 * NB * CPB)
            sp.wait_ge(s_ve, 2 * NB * CPB)
            sp.dma_start(x1[:, :, :], x_t).then_inc(s_xin, 16)
            wfc_v = wfc_d.rearrange("e (k p) f -> p (e k) f", p=P)
            wfc_s = wfc[:, :].rearrange("p (c f) -> p c f", f=FF)
            PIECES = 2 * E * KC
            HF = FF // 2

            def load_wfc(j):
                at = (slice(None), ds(j // 2, 1), ds((j % 2) * HF, HF))
                sp.dma_start(wfc_s[at], wfc_v[at]).then_inc(s_wfc, 16)

            for j in [0, 1] + list(range(2 * NGR, PIECES)):
                load_wfc(j)
            with sp.Fori(1, NGR) as p:
                for hl in range(4):
                    sp.wait_ge(s_ST, NC * (4 * p + hl - 3))
                    load_head(4 * p + hl, hl)
                    if hl % 2:
                        load_wfc(2 * p + hl // 2)

            sp.wait_ge(s_pv, NH * QT)
            for e in range(E):
                sp.dma_start(arena[:, e * WSTEP:(e + 1) * WSTEP].rearrange("p (c d) -> p c d", c=FC),
                             wproj_d[e].rearrange("(c p) d -> p c d", p=P)).then_inc(s_wp, 16)

            sp.wait_ge(s_sc, 16 * TT * TOPK)
            for s in range(2):
                sp.dma_start(xslot[s], xs_d[s * P:(s + 1) * P, :]).then_inc(s_xs[s], 16)

            def store_tile(t, s):
                sp.wait_ge(s_yo, t + 1)
                sp.dma_start(ys_d[ds(t * P, P), :], yslot[s]).then_inc(s_ys[s], 16)

            def load_tile(t, s):
                sp.wait_ge(s_mt, t - 1)
                sp.dma_start(xslot[s], xs_d[ds(t * P, P), :]).then_inc(s_xs[s], 16)

            NL = (NT - 3) // 2
            with sp.Fori(0, NL) as q:
                for s in range(2):
                    load_tile(2 * q + 2 + s, s)
                    store_tile(2 * q + s, s)
            for t in range(2 * NL + 2, NT):
                load_tile(t, t % 2)
            for t in range(2 * NL, NT):
                store_tile(t, t % 2)

            with sp.Fori(0, TT // NG) as g:
                for j in range(NG):
                    sp.wait_ge(s_o, NG * g + j + 1)
                    sp.dma_start(out_t[:, ds(NG * g + j, 1), :], ct[j][:, 1:2, :]).then_inc(s_out[j], 16)
            for j in range(NG):
                sp.wait_ge(s_out[j], 16 * TT // NG)

        @block.gpsimd
        def _(pool):
            pool.memset(ident[:, :], 0.0).then_inc(s_const, 1)
            pool.memset(lower[:, :], 1.0).then_inc(s_const, 1)
            pool.memset(tle[:, :, :], 1.0).then_inc(s_const, 1)
            pool.memset(ones[:, :], 1.0).then_inc(s_const, 1)
            pool.memset(causal[:, :], 1.0).then_inc(s_const, 1)
            pool.memset(identb[:, :], 0.0).then_inc(s_const, 1)
            pool.memset(dmask[:, :], 0.0).then_inc(s_const, 1)
            pool.memset(zero8[:, :], 0.0).then_inc(s_const, 1)
            for s in range(2):
                pool.memset(vh[s], 1.0).then_inc(s_const, 1)
            for s in range(4):
                pool.memset(ks[s], 1.0).then_inc(s_const, 1)
            pool.memset(cst0[:, :], 0.0).then_inc(s_zero, 1)
            pool.memset(zero, 0.0).then_inc(s_zero, 1)
            pool.iota(iota_e[:, :], [[1, E]], base=0, channel_multiplier=0,
                      allow_small_or_imprecise_dtypes=True).then_inc(s_const, 1)
            pool.iota(thr[:, :], [[P, TT]], base=0, channel_multiplier=0,
                      allow_small_or_imprecise_dtypes=True).then_inc(s_const, 1)
            pool.iota(iota_t[:, :], [[1, NT]], base=0, channel_multiplier=0,
                      allow_small_or_imprecise_dtypes=True).then_inc(s_const, 1)
            pool.wait_ge(s_const, 17)
            pool.affine_select(out=ident[:, :], in_=ident[:, :], compare_op=ALU.not_equal, fill=1.0,
                               base=0, pattern=[[-1, P]], channel_multiplier=1).then_inc(s_ident, 1)
            pool.affine_select(out=lower[:, :], in_=lower[:, :], compare_op=ALU.is_gt, fill=0.0,
                               base=0, pattern=[[1, P]], channel_multiplier=-1).then_inc(s_const, 1)
            pool.affine_select(out=causal[:, :], in_=causal[:, :], compare_op=ALU.is_ge, fill=0.0, base=0,
                               pattern=[[1, P]], channel_multiplier=-1).then_inc(s_const, 1)
            pool.affine_select(out=identb[:, :], in_=identb[:, :], compare_op=ALU.not_equal, fill=1.0,
                               base=0, pattern=[[-1, P]], channel_multiplier=1).then_inc(s_const, 1)
            for part in range(3):
                if part:
                    pool.wait_ge(s_const, 20 + part)
                pool.affine_select(out=dmask[:, :], in_=dmask[:, :], compare_op=ALU.not_equal, fill=1.0,
                                   base=-MROW - QT * part, pattern=[[-1, QT]],
                                   channel_multiplier=1).then_inc(s_const, 1)
            pool.affine_select(out=tle[:, :, :], in_=tle[:, :, :], compare_op=ALU.is_ge, fill=0.0,
                               base=0, pattern=[[1, E], [-1, E]], channel_multiplier=0).then_inc(s_const, 1)
            def split(b, cc):
                for g in range(4):
                    n = 4 * (CPB * b + cc) + g
                    pool.wait_ge(s_p2, n + 1)
                    pool.tensor_tensor(parts[g][:, 2, :], resid[g % 2], parts[g][:, 1, :],
                                       ALU.subtract).then_inc(s_p3, 1)

            with pool.Fori(0, NB) as b:
                for cc in range(CPB):
                    split(b, cc)

            pool.wait_ge(s_zero, 2)
            for t in range(0, NT, 8):
                n = min(8, NT - t)
                pool.dma_start(xs_d[t * P:(t + n) * P, :].rearrange("(t p) d -> p t d", p=P),
                               zero.unsqueeze(1).to_broadcast([P, n, D])).then_inc(s_xsz, 16)

            pool.wait_ge(s_const, 23)

            def body(p, ks_, first, tail):
                for k in ks_:
                    if k % QT == 0 and live(k - QT, first, tail):
                        hl = k // QT - 1
                        h, s = 4 * p + hl, hl % 2
                        nm, parts_ = negmax[:, s, :], mparts[:, s]
                        pool.wait_ge(s_max, QT * h + QT)
                        wait_pos(pool, s_mtp, h - 1)
                        pool.tensor_tensor(parts_[:, 0, :], nm, zero8[:, :], ALU.add).then_inc(s_sp, 1)
                        pool.wait_ge(s_sp, 4 * h + 1)
                        pool.tensor_tensor(mres[:, s, :], nm, parts_[:, 0, :], ALU.subtract).then_inc(s_sp, 1)
                        pool.wait_ge(s_sp, 4 * h + 2)
                        pool.tensor_tensor(parts_[:, 1, :], mres[:, s, :], zero8[:, :], ALU.add).then_inc(s_sp, 1)
                        pool.wait_ge(s_sp, 4 * h + 3)
                        pool.tensor_tensor(parts_[:, 2, :], mres[:, s, :], parts_[:, 1, :],
                                           ALU.subtract).then_inc(s_sp, 1)
                    if (k - LAG_E) % QT == 0 and live(k - LAG_E, first, tail):
                        hl = (k - LAG_E) // QT
                        h = 4 * p + hl
                        wait_pos(pool, s_pv, QT * (h - 1))
                        wait_pos(pool, s_mask, U * p + k - LAG_B)
                        pool.wait_ge(s_mtc, h + 1)
                        pool.tensor_tensor(qs[hl % 4][MROW:MROW + MR, :].rearrange("p (i q) -> p i q", i=QT),
                                           mT[MROW:MROW + MR, :].unsqueeze(1).to_broadcast([MR, QT, P]),
                                           dmask[MROW:MROW + MR, :].unsqueeze(2).to_broadcast([MR, QT, P]),
                                           ALU.mult).then_inc(s_ex, 1)
                        pool.wait_ge(s_ex, h + 1)
                        pool.tensor_copy(vh[hl % 2][:, :, 0:DH], v_sb[:, ds(h * QT * DH, QT * DH)]
                                         .rearrange("p (i d) -> p i d", d=DH)).then_inc(s_vc, 1)
                    if live(k - LAG_B, first, tail):
                        hl, i = divmod(k - LAG_B, QT)
                        h = 4 * p + hl
                        _, _, _, n = of_tile[i][0]
                        pool.wait_ge(s_expB, NC * h + n + 1)
                        blk = et_sb[n % NET][:, 0:P]
                        pool.tensor_tensor(blk, blk, causal[:, :], ALU.mult).then_inc(s_mask, 1)

            groups(pool, body)

            pool.wait_ge(s_xin, 16)
            with pool.Fori(0, TT // TPC) as g:
                pool.wait_ge(s_y2, g + 1)
                pool.tensor_tensor(x1[:, ds(g * TPC, TPC), :], x1[:, ds(g * TPC, TPC), :],
                                   yx[:, ds(g * TPC, TPC), :], ALU.add).then_inc(s_add, 1)

            pool.wait_ge(s_pos, 1)
            pool.wait_ge(s_xsz, 16 * ((NT + 7) // 8))
            pool.wait_ge(s_x2, TT // TPC)
            for t in range(TT):
                for j in range(TOPK):
                    pool.indirect_dma_start(out=xs_d, out_offset=bass.IndirectOffsetOnAxis(ap=pos[:, j, t:t + 1], axis=0),
                                            in_=yx[:, t, :], in_offset=None).then_inc(s_sc, 16)

            for s in range(2):
                pool.wait_ge(s_ys[s], 16 * ((NT + 1 - s) // 2))
            for t in range(TT):
                if t >= NG:
                    pool.wait_ge(s_o, t - NG + 1)
                    pool.wait_ge(s_out[t % NG], 16 * (t // NG))
                for j in range(TOPK):
                    pool.indirect_dma_start(out=ct[t % NG][:, j, :], out_offset=None, in_=ys_d,
                                            in_offset=bass.IndirectOffsetOnAxis(ap=pos[:, j, t:t + 1], axis=0))\
                        .then_inc(s_g[t % NG], 16)

        @block.scalar
        def _(act):
            act.wait_ge(s_zero, 1)
            nc.scalar.activation(warm[:, 0:1], cst0[:, 0:1], ACT.Sqrt).then_inc(s_warm, 1)

            def project(b, cc):
                c = CPB * b + cc
                act.wait_ge(s_var, c + 1)
                nc.scalar.activation(std[:, cc, :], mv[:, cc, :, 1], ACT.Sqrt).then_inc(s_std, 1)
                act.wait_ge(s_xt, KC * c + 1)
                if not isinstance(c, int) or c >= 2:
                    act.wait_ge(s_v, 2 * (c - 1))
                nc.scalar.copy(xnT[cc][:, 0, :], bk(0)).then_inc(s_xta, 1)
                for g in range(4):
                    act.wait_ge(s_qk, 4 * c + g + 1)
                    if not isinstance(c, int) or c >= 1:
                        act.wait_ge(s_st[g], 16 * c)
                    nc.scalar.mul(parts[g][:, 0, :], bk(2 + g), Q_SCALE if g < KC else 1.0).then_inc(s_p1, 1)
                for j in range(2):
                    act.wait_ge(s_v, 2 * c + j + 1)
                    for t in range(2):
                        i = TPC * cc + 2 * j + t
                        dst = v_sb.rearrange("p (b h i d) -> p b h i d", b=NB, h=H, i=QT)[:, ds(b, 1), :, i, :]
                        ins = nc.scalar.copy(dst, bk(6 + j)[:, t * D:(t + 1) * D]
                                             .rearrange("p (b h d) -> p b h d", b=1, h=H))
                    ins.then_inc(s_ve, 1)

            for cc in range(CPB):
                project(0, cc)
            if NB > 1:
                with act.Fori(1, NB) as b:
                    for cc in range(CPB):
                        project(b, cc)
            act.wait_ge(s_warm, 1)
            nc.scalar.activation(warm[:, 1:2], cst0[:, 0:1], ACT.Exp).then_inc(s_warm, 1)

            def body(p, ks_, first, tail):
                for k in ks_:
                    if (k - LAG_M) % QT == 0 and live(k - LAG_M, first, tail):
                        hl = (k - LAG_M) // QT
                        h = 4 * p + hl
                        act.wait_ge(s_mtp, h + 1)
                        wait_pos(act, s_ex, h)
                        nc.scalar.copy(mT[MROW:MROW + MR, :],
                                       bk(ebank("m", k, hl, 0))[MROW:MROW + MR, 0:P]).then_inc(s_mtc, 1)
                    if live(k - LAG_B, first, tail):
                        hl, i = divmod(k - LAG_B, QT)
                        h = 4 * p + hl
                        for (_, q0, nq, n) in of_tile[i]:
                            act.wait_ge(s_ST, NC * h + n + 1)
                            hb, nb = divmod(n - NET, NC)
                            wait_pos(act, s_pv, QT * (h + hb) + chunks[nb][0] + 1)
                            nc.scalar.activation(et_sb[n % NET][:, 0:nq], bk(ebank("s", k, hl, n))[:, 0:nq],
                                                 ACT.Exp).then_inc(s_expB, 1)
                    if not tail:
                        hl, i = divmod(k, QT)
                        act.wait_ge(s_max, U * p + k + 1)
                        if i == 0:
                            wait_pos(act, s_denc, 4 * p + hl - 3)
                        sc = ps[:, 2 * (k % 2):2 * (k % 2) + 2, :].rearrange("p b q -> p (b q)")[:, i * P:N]
                        nc.scalar.activation(sc, sc, ACT.Exp, bias=negmax[:, hl % 2, i:i + 1],
                                             accum_out=den[:, hl, i:i + 1]).then_inc(s_exp, 1)

            groups(act, body)

            act.wait_ge(s_warm, 2)
            act.wait_ge(s_xsz, 16 * ((NT + 7) // 8))
            nc.scalar.activation(warm[:, 0:1], cst0[:, 0:1], ACT.Sqrt).then_inc(s_warm, 1)
            def root_y(g):
                act.wait_ge(s_vary, g + 1)
                nc.scalar.activation(std[:, 0, :], mv[:, 0, :, 1], ACT.Sqrt).then_inc(s_stdy, 1)

            def root_x(g):
                act.wait_ge(s_varx, g + 1)
                nc.scalar.activation(std[:, 1, :], mv[:, 1, :, 1], ACT.Sqrt).then_inc(s_stdx, 1)

            def copy_x2(g):
                for kc in range(KC):
                    act.wait_ge(s_x2t, KC * g + kc + 1)
                    nc.scalar.copy(x2T[:, kc, :], bk(kc)).then_inc(s_x2e, 1)

            G = TT // TPC
            root_y(0)
            root_y(1)
            root_x(0)
            if G > 2:
                with act.Fori(2, G) as g:
                    root_y(g)
                    root_x(g - 1)
                    copy_x2(g - 2)
            root_x(G - 1)
            copy_x2(G - 2)
            copy_x2(G - 1)
            act.wait_ge(s_warm, 3)
            act.wait_ge(s_d2, 1)
            nc.scalar.activation(gtmp[:, :], gtmp[:, :], ACT.Exp).then_inc(s_ex2, 1)
            nc.scalar.activation(warm[:, 1:2], cst0[:, 0:1], ACT.Gelu).then_inc(s_warm, 1)

            def mix(t):
                for hf in range(2):
                    act.wait_ge(s_fc, 2 * t + hf + 1)
                    wait_pos(act, s_ht, 2 * t)
                    nc.scalar.activation(hid[:, hf * 512:(hf + 1) * 512], bk(1 + hf), ACT.Gelu).then_inc(s_ge, 1)
                act.wait_ge(s_ht, 2 * t + 1)
                wait_pos(act, s_pr, t)
                nc.scalar.copy(hidT[:, 0:4, :], bk(3).rearrange("p (c t) -> p c t", c=4)).then_inc(s_hea, 1)

            mix(0)
            with act.Fori(1, NT) as t:
                mix(t)

            act.wait_ge(s_warm, 4)
            nc.scalar.activation(warm[:, 0:1], cst0[:, 0:1], ACT.Sqrt).then_inc(s_warm, 1)
            with act.Fori(0, TT // 2) as q:
                for s in range(2):
                    act.wait_ge(s_var3, 2 * q + s + 1)
                    nc.scalar.activation(std[:, s, 0:1], mv[:, s, 0, 1:2], ACT.Sqrt).then_inc(s_std3, 1)
            act.wait_ge(s_warm, 5)

        @block.tensor
        def _(pe):
            pe.wait_ge(s_ident, 1)
            pe.wait_ge(s_w, 64)

            def project(b, cc):
                c = CPB * b + cc
                pe.wait_ge(s_xn, c + 1)
                for kc in range(KC):
                    wait_pos(pe, (s_xta, s_xtd)[kc], c)
                    for t in range(TPC):
                        ins = nc.tensor.transpose(bk(kc)[:, t * P:(t + 1) * P], xc[cc][:, t, kc * P:(kc + 1) * P],
                                                  ident[:, :])
                    ins.then_inc(s_xt, 1)
                pe.wait_ge(s_xta, c + 1)
                pe.wait_ge(s_xtd, c + 1)
                for g in range(4):
                    wait_pos(pe, s_res, 4 * c + g - 3)
                    ty, cg = divmod(g, KC)
                    for kc in range(KC):
                        ins = nc.tensor.matmul(bk(2 + g), wqkv[:, ty, kc, cg * P:(cg + 1) * P], xnT[cc][:, kc, :],
                                               start=(kc == 0), stop=(kc == KC - 1))
                    ins.then_inc(s_qk, 1)
                for j in range(2):
                    wait_pos(pe, s_ve, 2 * c + j - 1)
                    for t in range(2):
                        for kc in range(KC):
                            ins = nc.tensor.matmul(bk(6 + j)[:, t * D:(t + 1) * D],
                                                   xnT[cc][:, kc, (2 * j + t) * P:(2 * j + t + 1) * P],
                                                   wqkv[:, 2, kc, :], start=(kc == 0), stop=(kc == KC - 1))
                    ins.then_inc(s_v, 1)

            for cc in range(CPB):
                project(0, cc)
            if NB > 1:
                with pe.Fori(1, NB) as b:
                    for cc in range(CPB):
                        project(b, cc)
            pe.wait_ge(s_res, 4 * NB * CPB)
            pe.wait_ge(s_ve, 2 * NB * CPB)

            def body(p, ks_, first, tail):
                for k in ks_:
                    if k in STEP_T and not first:
                        b = STEP_T.index(k)
                        ev = ("t", k, -4, b)
                        free_bank(pe, p, first, tail, ev)
                        pe.wait_ge(s_poc, 2 * p - 1 + b)
                        for t in range(4):
                            ins = nc.tensor.transpose(bk(ebank(*ev))[:, t * P:(t + 1) * P],
                                                      po_sb[:, (4 * b + t) * P:(4 * b + t + 1) * P], ident[:, :])
                        ins.then_inc(s_T4, 1)
                    if not tail:
                        hl, i = divmod(k, QT)
                        if i == 0:
                            pe.wait_ge(s_ld[hl], 16 * 2 * TERMS * (p + 1))
                        wait_pos(pe, s_exp, U * p + k - 1)
                        for hf in range(2):
                            ins = nc.tensor.matmul(bk(2 * (k % 2) + hf), qs[hl][0:SROWS, i * P:(i + 1) * P],
                                                   ks[hl][0:SROWS, hf * 512:(hf + 1) * 512], start=True, stop=True)
                        ins.then_inc(s_S, 1)
                    if (k - LAG_M) % QT == 0 and live(k - LAG_M, first, tail):
                        hl = (k - LAG_M) // QT
                        h = 4 * p + hl
                        free_bank(pe, p, first, tail, ("m", k, hl, 0))
                        pe.wait_ge(s_sp, 4 * h + 4)
                        nc.tensor.matmul(bk(ebank("m", k, hl, 0))[MROW:MROW + MR, 0:P],
                                         mparts[:, hl % 2].rearrange("p s i -> p (s i)"), identb[:, :],
                                         start=True, stop=True).then_inc(s_mtp, 1)
                    if live(k - LAG_B, first, tail):
                        hl, i = divmod(k - LAG_B, QT)
                        h = 4 * p + hl
                        if i == 0:
                            pe.wait_ge(s_ex, h + 1)
                        for (_, q0, nq, n) in of_tile[i]:
                            free_bank(pe, p, first, tail, ("s", k, hl, n))
                            nc.tensor.matmul(bk(ebank("s", k, hl, n))[:, 0:nq],
                                             ks[hl % 4][0:MROW + MR, i * P:(i + 1) * P],
                                             qs[hl % 4][0:MROW + MR, q0:q0 + nq],
                                             start=True, stop=True).then_inc(s_ST, 1)
                    if live(k - LAG_P, first, tail):
                        hl, i = divmod(k - LAG_P, QT)
                        h, j = 4 * p + hl, 32 * (hl % 4)
                        if i == 0:
                            pe.wait_ge(s_vc, h + 1)
                        for (_, q0, nq, n) in of_tile[i]:
                            pe.wait_ge(s_expB, NC * h + n + 1)
                            out, et = bk(6 + q0 // 512), et_sb[n % NET]
                            if i == 0 and hl == 0:
                                wait_pos(pe, s_poc, 2 * p - 1 + q0 // 512)
                            q = q0 % 512
                            diag = P if q0 == i * P else 0
                            if nq > diag:
                                ins = nc.tensor.matmul(out[j:j + VW, q + diag:q + nq], vh[hl % 2][:, i, :],
                                                       et[:, diag:nq], start=(i == 0), stop=False,
                                                       skip_group_check=True)
                            if diag:
                                pe.wait_ge(s_mask, QT * h + i + 1)
                                ins = nc.tensor.matmul(out[j:j + DH, q:q + P], vh[hl % 2][:, i, 0:DH], et[:, 0:P],
                                                       start=False, stop=False, skip_group_check=True)
                        ins.then_inc(s_pv, 1)

            pe.wait_ge(s_poz, 1)
            pe.wait_ge(s_const, 23)
            groups(pe, body)

            pe.wait_ge(s_expB, NC * NH)
            pe.wait_ge(s_exp, QT * NH)
            pe.wait_ge(s_norm, 2 * NGR)

            def route(g):
                pe.wait_ge(s_x2, g + 1)
                for kc in range(KC):
                    wait_pos(pe, s_x2e, KC * g + kc - 1)
                    for t in range(TPC):
                        ins = nc.tensor.transpose(bk(kc)[:, t * P:(t + 1) * P],
                                                  yx[:, g * TPC + t, kc * P:(kc + 1) * P], ident[:, :])
                    ins.then_inc(s_x2t, 1)
                pe.wait_ge(s_x2e, KC * (g + 1))
                for t in range(TPC):
                    for kc in range(KC):
                        ins = nc.tensor.matmul(bk(2)[:, (g * TPC + t) * E:(g * TPC + t + 1) * E],
                                               x2T[:, kc, t * P:(t + 1) * P], router[:, kc, :],
                                               start=(kc == 0), stop=(kc == KC - 1))
                ins.then_inc(s_lg, 1)

            for g in range(TT // TPC):
                route(g)

            pe.wait_ge(s_oh, 1)
            pe.wait_ge(s_const, 23)
            rank = bk(3)[:, 0:(TT + 1) * E].rearrange("p (t e) -> p t e", e=E)
            nc.tensor.matmul(rank[:, 0:TT, :], lower[:, :], oh_bf[:, :, :], start=True, stop=False,
                             skip_group_check=True)
            for t in range(TT):
                n = TT - t
                ins = nc.tensor.matmul(rank[:, t + 1:TT + 1, :], ones[:, :],
                                       oh_bf[:, t, :].unsqueeze(1).to_broadcast([P, n, E]),
                                       start=False, stop=(t == TT - 1), skip_group_check=True)
            ins.then_inc(s_rank, 1)

            pe.wait_ge(s_tab, 1)
            pe.wait_ge(s_wfc, 16 * 2 * E * KC)

            def transpose_x(t, s):
                pe.wait_ge(s_xs[s], 16 * (t // 2 + 1) if isinstance(t, int) else t * 8 + 8 * (2 - s))
                wait_pos(pe, s_me, t)
                for kc in range(KC):
                    ins = nc.tensor.transpose(bk(0)[:, kc * P:(kc + 1) * P], xslot[s][:, kc * P:(kc + 1) * P],
                                              ident[:, :])
                ins.then_inc(s_mt, 1)

            def first_product(t, off):
                pe.wait_ge(s_me, t + 1)
                for hf in range(2):
                    wait_pos(pe, s_ge, 2 * t + hf - 1)
                    for kc in range(KC):
                        ins = nc.tensor.matmul(bk(1 + hf), xsT[:, kc, :],
                                               wfc[:, ds(off + (kc * FF + hf * 512), 512)],
                                               start=(kc == 0), stop=(kc == KC - 1))
                    ins.then_inc(s_fc, 1)

            def transpose_h(t):
                for hf in range(2):
                    pe.wait_ge(s_ge, 2 * t + hf + 1)
                    wait_pos(pe, (s_hea, s_hed)[hf], t)
                    for c in range(4):
                        ins = nc.tensor.transpose(bk(3 + hf)[:, c * P:(c + 1) * P],
                                                  hid[:, (4 * hf + c) * P:(4 * hf + c + 1) * P], ident[:, :])
                    ins.then_inc(s_ht, 1)

            def second_product(t, s, off):
                wait_pos(pe, s_yo, t - 1)
                pe.wait_ge(s_hea, t + 1)
                for c in range(FC):
                    if c == FC // 2:
                        pe.wait_ge(s_hed, t + 1)
                    ins = nc.tensor.matmul(bk(5 + s)[:, 0:D], hidT[:, c, :], arena[:, ds(off + c * D, D)],
                                           start=(c == 0), stop=(c == FC - 1))
                ins.then_inc(s_pr, 1)

            def expert(t):
                return pe.value_load(tab[0:1, ds(t, 1)], min_val=0, max_val=(E - 1) * WSTEP)

            def step(t, s, first=False, last=False):
                if not first:
                    transpose_h(t - 1)
                if not last:
                    first_product(t, expert(t))
                    if not (isinstance(t, int) and t == NT - 1):
                        transpose_x(t + 1, 1 - s)
                if not first:
                    second_product(t - 1, 1 - s, expert(t - 1))

            transpose_x(0, 0)
            step(0, 0, first=True)
            pe.wait_ge(s_wp, 16 * E)
            step(1, 1)
            step(2, 0)
            NL2 = (NT - 4) // 2
            with pe.Fori(0, NL2) as q:
                step(2 * q + 3, 1)
                step(2 * q + 4, 0)
            for t in range(2 * NL2 + 3, NT):
                step(t, t % 2)
            step(NT, NT % 2, last=True)

        @block.vector
        def _(dve):
            def ln_stats(src, s, n, s_chain, chain0, s_out_):
                for t in range(n):
                    nc.vector.bn_stats(stats[:, s, t, :], src[t]).then_inc(s_chain, 1)
                dve.wait_ge(s_chain, chain0 + n)
                nc.vector.memset(pause[:, :], 0.0)
                for t in range(n):
                    nc.vector.bn_aggr(mv[:, s, t, :], stats[:, s, t, :]).then_inc(s_chain, 1)
                dve.wait_ge(s_chain, chain0 + 2 * n)
                nc.vector.tensor_scalar(mv[:, s, 0:n, 1], mv[:, s, 0:n, 1], EPS, None, ALU.add).then_inc(s_out_, 1)

            def ln_apply(dst, src, s, n, s_chain, chain1):
                nc.vector.reciprocal(rstd[:, s, 0:n], std[:, s, 0:n]).then_inc(s_chain, 1)
                dve.wait_ge(s_chain, chain1)
                for t in range(n):
                    ins = nc.vector.tensor_scalar(dst[t], src[t], mv[:, s, t, 0:1], rstd[:, s, t:t + 1],
                                                  ALU.subtract, ALU.mult)
                return ins

            CH = 2 * TPC + 1

            def project(b, cc):
                c = CPB * b + cc
                dve.wait_ge(s_x[cc], 16 * (b + 1))
                rows = [xc[cc][:, t, :] for t in range(TPC)]
                ln_stats(rows, cc, TPC, s_bn, CH * c, s_var)
                dve.wait_ge(s_std, c + 1)
                ln_apply(rows, rows, cc, TPC, s_bn, CH * (c + 1)).then_inc(s_xn, 1)
                dve.wait_ge(s_xt, KC * (c + 1))
                if not isinstance(c, int) or c >= 2:
                    dve.wait_ge(s_v, 2 * (c - 1))
                nc.vector.tensor_copy(xnT[cc][:, 1, :], bk(1)).then_inc(s_xtd, 1)
                for g in range(4):
                    dve.wait_ge(s_p1, 4 * c + g + 1)
                    wait_pos(dve, s_p3, 4 * c + g - 1)
                    nc.vector.scalar_tensor_tensor(out=resid[g % 2], in0=bk(2 + g),
                                                   scalar=Q_SCALE if g < KC else 1.0, in1=parts[g][:, 0, :],
                                                   op0=ALU.mult, op1=ALU.subtract).then_inc(s_res, 1)
                    dve.wait_ge(s_res, 4 * c + g + 1)
                    if not isinstance(c, int) or c >= 1:
                        dve.wait_ge(s_st[g], 16 * c)
                    nc.vector.tensor_copy(parts[g][:, 1, :], resid[g % 2]).then_inc(s_p2, 1)

            for cc in range(CPB):
                project(0, cc)
            if NB > 1:
                with dve.Fori(1, NB) as b:
                    for cc in range(CPB):
                        project(b, cc)

            dve.wait_ge(s_ve, 2 * NB * CPB)
            nc.vector.memset(ps[:, 6:8, :], 0.0).then_inc(s_poz, 1)

            def body(p, ks_, first, tail):
                for k in ks_:
                    if k in STEP_T and not first:
                        b = STEP_T.index(k)
                        dve.wait_ge(s_T4, 2 * p - 1 + b)
                        nc.vector.tensor_copy(po_sb[:, b * 512:(b + 1) * 512],
                                              bk(ebank("t", k, -4, b))).then_inc(s_oc, 1)
                    if not tail:
                        hl, i = divmod(k, QT)
                        dve.wait_ge(s_S, U * p + k + 1)
                        if i == 0:
                            wait_pos(dve, s_sp, 4 * (4 * p + hl - 1))
                        nc.vector.tensor_reduce(negmax[:, hl % 2, i:i + 1], ps[:, 2 * (k % 2):2 * (k % 2) + 2, :],
                                                AX.XY, ALU.max, negate=True).then_inc(s_max, 1)
                    for b in range(2):
                        o4 = po_sb[:, b * 512:(b + 1) * 512].rearrange("p (i h r) -> p i h r", i=4, h=4)
                        sl = slice(4 * b, 4 * b + 4)
                        if first or not STEP_N[b] <= k <= STEP_N[b] + 2:
                            continue
                        if k == STEP_N[b]:
                            dve.wait_ge(s_denc, 4 * p)
                            dve.wait_ge(s_oc, 2 * p - 1 + b)
                            nc.vector.tensor_tensor(den_t[:, sl, :], o4[:, :, :, DH],
                                                    den_u[:, :, sl].rearrange("p h i -> p i h"),
                                                    ALU.add).then_inc(s_nc, 1)
                        elif k == STEP_N[b] + 1:
                            dve.wait_ge(s_nc, 4 * p - 3 + 2 * b)
                            nc.vector.reciprocal(rden[:, sl, :], den_t[:, sl, :]).then_inc(s_nc, 1)
                        else:
                            dve.wait_ge(s_nc, 4 * p - 2 + 2 * b)
                            hh, bb = (4 * (p - 1)) % H, (4 * (p - 1)) // H
                            dst = yx[:, ds(bb * QT + 4 * b, 4), ds(hh * DH, 4 * DH)]
                            nc.vector.tensor_tensor(dst.rearrange("p i (h d) -> p i h d", h=4), o4[:, :, :, 0:DH],
                                                    rden[:, sl, :].unsqueeze(3).to_broadcast([P, 4, 4, DH]),
                                                    ALU.mult).then_inc(s_norm, 1)
                    if k in STEP_C and not first:
                        b = STEP_C.index(k)
                        dve.wait_ge(s_pv, U * p - 4 * (1 - b))
                        nc.vector.tensor_copy(po_sb[:, b * 512:(b + 1) * 512], bk(6 + b)).then_inc(s_poc, 1)
                    if (k - STEP_D) % QT == 0 and live(k - STEP_D, first, tail):
                        hl = (k - STEP_D) // QT
                        dve.wait_ge(s_exp, QT * (4 * p + hl + 1))
                        nc.vector.tensor_copy(den_u[:, hl % 4, :], den[:, hl % 4, :]).then_inc(s_denc, 1)

            groups(dve, body)
            dve.wait_ge(s_norm, 2 * NGR)

            dve.wait_ge(s_xin, 16)
            G = TT // TPC

            def rows(buf, g):
                return [buf[:, ds(g * TPC + t, 1), :] for t in range(TPC)]

            def stats_y(g):
                ln_stats(rows(yx, g), 0, TPC, s_bny, CH * g, s_vary)

            def apply_y(g):
                dve.wait_ge(s_stdy, g + 1)
                ln_apply(rows(yx, g), rows(yx, g), 0, TPC, s_bny, CH * (g + 1)).then_inc(s_y2, 1)

            def stats_x(g):
                dve.wait_ge(s_add, g + 1)
                ln_stats(rows(x1, g), 1, TPC, s_bnx, CH * g, s_varx)

            def apply_x(g):
                dve.wait_ge(s_stdx, g + 1)
                ln_apply(rows(yx, g), rows(x1, g), 1, TPC, s_bnx, CH * (g + 1)).then_inc(s_x2, 1)

            stats_y(0)
            apply_y(0)
            with dve.Fori(1, G) as g:
                stats_y(g)
                stats_x(g - 1)
                apply_y(g)
                apply_x(g - 1)
            stats_x(G - 1)
            apply_x(G - 1)

            n_r = [0]

            def link(ins):
                n_r[0] += 1
                ins.then_inc(s_r, 1)
                dve.wait_ge(s_r, n_r[0])

            dve.wait_ge(s_lg, TT // TPC)
            link(nc.vector.tensor_copy(lg[:, :, :].rearrange("p t e -> p (t e)"), bk(2)[:, 0:TT * E]))
            for t in range(TT):
                ins = nc.vector.max(top[:, t, :], lg[:, t, :])
            link(ins)
            for t in range(TT):
                ins = nc.vector.max_index(topi[:, t, :], top[:, t, :], lg[:, t, :])
            link(ins)
            nc.vector.tensor_tensor(gtmp[:, :], top[:, :, 1], top[:, :, 0], ALU.subtract).then_inc(s_d2, 1)
            for j in range(TOPK):
                ins = nc.vector.tensor_copy(choice[:, j, :], topi[:, :, j])
            link(ins)
            dve.wait_ge(s_const, 23)
            for j in range(TOPK):
                ins = nc.vector.tensor_tensor(oh[:, j, :, :], choice[:, j, :].unsqueeze(2).to_broadcast([P, TT, E]),
                                              iota_e[:, :].unsqueeze(1).to_broadcast([P, TT, E]), ALU.is_equal)
            link(ins)
            nc.vector.tensor_tensor(oh_bf[:, :, :], oh[:, 0], oh[:, 1], ALU.add).then_inc(s_oh, 1)
            dve.wait_ge(s_ex2, 1)
            link(nc.vector.tensor_scalar(gate[:, 1, :], gtmp[:, :], 1.0, None, ALU.add))
            link(nc.vector.reciprocal(gate[:, 0, :], gate[:, 1, :]))
            link(nc.vector.tensor_tensor(gate[:, 1, :], gate[:, 0, :], gtmp[:, :], ALU.mult))
            dve.wait_ge(s_rank, 1)
            rank = bk(3)[:, 0:(TT + 1) * E].rearrange("p (t e) -> p t e", e=E)
            link(nc.vector.tensor_copy(cnt[:, :], rank[:, TT, :]))
            link(nc.vector.tensor_tensor(tmp_t[:, :, :], cnt[:, :].unsqueeze(2).to_broadcast([P, E, TT]),
                                         thr[:, :].unsqueeze(1).to_broadcast([P, E, TT]), ALU.is_gt))
            link(nc.vector.tensor_reduce(ntile[:, :], tmp_t[:, :, :], AX.X, ALU.add))
            link(nc.vector.tensor_tensor(tmp_e[:, :, :], tle[:, :, :], ntile[:, :].unsqueeze(1).to_broadcast([P, E, E]),
                                         ALU.mult))
            link(nc.vector.tensor_reduce(endt[:, :], tmp_e[:, :, :], AX.X, ALU.add))
            link(nc.vector.tensor_tensor(base[:, :], endt[:, :], ntile[:, :], ALU.subtract))
            link(nc.vector.tensor_scalar(base[:, :], base[:, :], float(P), None, ALU.mult))
            link(nc.vector.tensor_tensor(tmp[:, :, :], rank[:, 0:TT, :], base[:, :].unsqueeze(1).to_broadcast([P, TT, E]),
                                         ALU.add))
            for j in range(TOPK):
                ins = nc.vector.tensor_tensor(oh[:, j], oh[:, j], tmp[:, :, :], ALU.mult)
            link(ins)
            for j in range(TOPK):
                ins = nc.vector.tensor_reduce(posf[:, j, :], oh[:, j], AX.X, ALU.add)
            link(ins)
            nc.vector.tensor_copy(pos[:, :, :], posf[:, :, :]).then_inc(s_pos, 1)
            link(nc.vector.tensor_tensor(tmp_n[:, :, :], endt[0:1, :].unsqueeze(1).to_broadcast([1, NT, E]),
                                         iota_t[:, :].unsqueeze(2).to_broadcast([1, NT, E]), ALU.is_le))
            link(nc.vector.tensor_reduce(tabf[:, :], tmp_n[:, :, :], AX.X, ALU.add))
            link(nc.vector.tensor_scalar(tabf[:, :], tabf[:, :], float(E - 1), float(WSTEP), ALU.min, ALU.mult))
            nc.vector.tensor_copy(tab[:, :], tabf[:, :]).then_inc(s_tab, 1)

            def copy_x(t):
                dve.wait_ge(s_mt, t + 1)
                wait_pos(dve, s_fc, 2 * t)
                nc.vector.tensor_copy(xsT[:, :, :], bk(0)[:, 0:KC * P].rearrange("p (k t) -> p k t", k=KC))\
                  .then_inc(s_me, 1)

            def copy_h(t):
                dve.wait_ge(s_ht, 2 * t + 2)
                wait_pos(dve, s_pr, t)
                nc.vector.tensor_copy(hidT[:, 4:8, :], bk(4).rearrange("p (c t) -> p c t", c=4)).then_inc(s_hed, 1)

            def copy_y(t, s):
                dve.wait_ge(s_pr, t + 1)
                if not isinstance(t, int) or t >= 2:
                    dve.wait_ge(s_ys[s], 16 * (t // 2) if isinstance(t, int) else 8 * t - 8 * s)
                nc.vector.tensor_copy(yslot[s], bk(5 + s)[:, 0:D]).then_inc(s_yo, 1)

            def mix(t, s):
                if not isinstance(t, int) or t >= 1:
                    copy_h(t - 1)
                if not isinstance(t, int) or t < NT - 1:
                    copy_x(t + 1)
                if not isinstance(t, int) or t >= 1:
                    copy_y(t - 1, 1 - s)

            copy_x(0)
            mix(0, 0)
            mix(1, 1)
            mix(2, 0)
            NL3 = (NT - 4) // 2
            with dve.Fori(0, NL3) as q:
                mix(2 * q + 3, 1)
                mix(2 * q + 4, 0)
            for t in range(2 * NL3 + 3, NT + 1):
                mix(t, t % 2)

            def combine(t, j, front, back):
                jn, f, b = (j + 1) % NG, (j + 1) % 2, j % 2
                y0, y1 = ct[jn][:, 0:1, :], ct[jn][:, 1:2, :]
                z0, z1 = ct[j][:, 0:1, :], ct[j][:, 1:2, :]
                tn = t + 1
                if front:
                    dve.wait_ge(s_g[jn], 32 * (tn // NG + 1) if isinstance(t, int) else
                                (32 // NG) * (tn - jn) + 32)
                    nc.vector.tensor_scalar(y0, y0, gate[:, 0, ds(tn, 1)], None, ALU.mult).then_inc(s_cf, 1)
                if back:
                    dve.wait_ge(s_std3, t + 1)
                    nc.vector.reciprocal(rstd[:, b, 0:1], std[:, b, 0:1]).then_inc(s_cb, 1)
                if front:
                    dve.wait_ge(s_cf, 4 * tn + 1)
                    nc.vector.scalar_tensor_tensor(out=y0, in0=y1, scalar=gate[:, 1, ds(tn, 1)], in1=y0,
                                                   op0=ALU.mult, op1=ALU.add).then_inc(s_cf, 1)
                if back:
                    dve.wait_ge(s_cb, 2 * t + 1)
                    nc.vector.tensor_scalar(z0, z0, mv[:, b, 0, 0:1], rstd[:, b, 0:1],
                                            ALU.subtract, ALU.mult).then_inc(s_cb, 1)
                if front:
                    dve.wait_ge(s_cf, 4 * tn + 2)
                    nc.vector.bn_stats(stats[:, f, 0, :], y0).then_inc(s_cf, 1)
                if back:
                    dve.wait_ge(s_cb, 2 * t + 2)
                    nc.vector.tensor_tensor(z1, z0, x1[:, ds(t, 1), :], ALU.add).then_inc(s_o, 1)
                if front:
                    dve.wait_ge(s_cf, 4 * tn + 3)
                    nc.vector.memset(pause[:, :], 0.0)
                    nc.vector.bn_aggr(mv[:, f, 0, :], stats[:, f, 0, :]).then_inc(s_cf, 1)
                    dve.wait_ge(s_cf, 4 * tn + 4)
                    nc.vector.tensor_scalar(mv[:, f, 0, 1:2], mv[:, f, 0, 1:2], EPS, None, ALU.add)\
                      .then_inc(s_var3, 1)

            combine(-1, NG - 1, True, False)
            if TT > NG:
                with dve.Fori(0, TT // NG - 1) as g:
                    for j in range(NG):
                        combine(NG * g + j, j, True, True)
            for j in range(NG):
                t = TT - NG + j
                combine(t, j, t + 1 < TT, True)


_INS = ['L0_attn_content', 'L0_attn_Wq', 'L0_attn_Wk', 'L0_attn_Wv', 'L0_ffn_router_w', 'L0_ffn_w_fc', 'L0_ffn_w_proj']


def kernel(**inputs):
    import numpy as _np
    import concourse.bacc as _bacc
    from concourse import mybir as _mybir
    from concourse.bass_utils import run_bass_kernel_spmd as _run

    nc = _bacc.Bacc("TRN2", target_bir_lowering=False, num_devices=1)
    arrays, args = {}, []
    for name in _INS:
        a = _np.ascontiguousarray(inputs[name])
        arrays[f"in_{name}"] = a
        args.append(nc.dram_tensor(f"in_{name}", a.shape, _mybir.dt.from_np(a.dtype), kind="ExternalInput").ap())
    shape = inputs[_INS[0]].shape
    args.append(nc.dram_tensor("out_0", shape, _mybir.dt.float32, kind="ExternalOutput").ap())
    sandwich(nc, *args)
    r = _run(nc, [arrays], core_ids=[0])
    return r.results[0]["out_0"]
```

```python
import concourse.bass as bass
from concourse import mybir
from contextlib import ExitStack


def sandwich(nc, x_d, wq_d, wk_d, wv_d, router_d, wfc_d, wproj_d, out_d):
    F32, BF16, I32, U32 = mybir.dt.float32, mybir.dt.bfloat16, mybir.dt.int32, mybir.dt.uint32
    ACT = mybir.ActivationFunctionType
    ALU = mybir.AluOpType
    AX = mybir.AxisListType
    ds = bass.ds

    P = 128
    NB, N, D = x_d.shape
    H, DH = 16, D // 16
    KC = D // P
    QT = N // P
    NH = NB * H
    TT = NB * QT
    E, _, FF = wfc_d.shape
    FC = FF // P
    TOPK = 2
    NT = TT * TOPK + E - 1
    REG = NB * N + P
    CT = 512
    TPC = CT // P
    CPB = N // CT
    TERMS = 6
    SROWS = TERMS * DH
    Q_SCALE = DH ** -0.5
    EPS = 1e-5
    WSTEP = KC * FF
    assert WSTEP == FC * D and CPB == 2 and N == 1024

    qk_d = nc.dram_tensor("qk_parts", [2, 3, NB * D, N], BF16, kind="Internal").ap()
    xs_d = nc.dram_tensor("expert_in", [E * REG, D], F32, kind="Internal").ap()
    ys_d = nc.dram_tensor("expert_out", [NT * P, D], F32, kind="Internal").ap()

    x_t = x_d.rearrange("b (i p) d -> p (b i) d", p=P)
    out_t = out_d.rearrange("b (i p) d -> p (b i) d", p=P)

    ctx = ExitStack()
    with ctx:
        def sb(name, shape, dt=F32):
            return ctx.enter_context(nc.sbuf_tensor(name, shape, dt))

        def sem(name):
            return ctx.enter_context(nc.semaphore(name))

        wfc = sb("wfc", [P, E * WSTEP])
        arena = sb("arena", [P, E * WSTEP])
        yx = sb("yx", [P, TT, D])
        x1 = sb("x1", [P, TT, D])

        KB = 256
        v_sb = arena[:, 0:NH * QT * DH]
        a0 = NH * QT * DH
        qs = [arena[:, a0 + s * 2 * KB:a0 + (s + 1) * 2 * KB].bitcast(BF16) for s in range(4)]
        a0 += 8 * KB
        ks = [arena[:, a0 + s * 2 * KB:a0 + (s + 1) * 2 * KB].bitcast(BF16) for s in range(4)]
        a0 += 8 * KB
        NET = 6
        et_sb = [arena[:, a0 + s * 512:a0 + (s + 1) * 512] for s in range(NET)]
        a0 += NET * 512
        VW = DH + 1
        vh = [arena[:, a0 + s * QT * VW:a0 + (s + 1) * QT * VW].rearrange("p (i d) -> p i d", d=VW) for s in range(2)]
        a0 += 2 * QT * VW
        assert a0 <= E * WSTEP

        yx_f = yx[:, :, :].rearrange("p t d -> p (t d)")
        x1_f = x1[:, :, :].rearrange("p t d -> p (t d)")
        if NB == 4:
            pa, pb = yx_f, x1_f
        else:
            pa = sb("pa", [P, 32 * KB])[:, :]
            pb = sb("pb", [P, 16 * KB])[:, :]
        xc = [pa[:, s * TPC * D:(s + 1) * TPC * D].rearrange("p (t d) -> p t d", d=D) for s in range(2)]
        o = 2 * TPC * D
        xnT = [pa[:, o + s * KC * CT:o + (s + 1) * KC * CT].rearrange("p (k t) -> p k t", k=KC) for s in range(2)]
        o += 2 * KC * CT
        wqkv = pa[:, o:o + 3 * KC * D].rearrange("p (w k d) -> p w k d", w=3, k=KC)
        parts = [pb[:, g * 3 * KB:(g + 1) * 3 * KB].bitcast(BF16).rearrange("p (s t) -> p s t", s=3)
                 for g in range(4)]
        o = 12 * KB
        resid = [pb[:, o + s * CT:o + (s + 1) * CT] for s in range(2)]

        ident = sb("ident", [P, P])
        stats = sb("stats", [P, 2, TPC, 6])
        mv = sb("mv", [P, 2, TPC, 2])
        std = sb("std", [P, 2, TPC])
        rstd = sb("rstd", [P, 2, TPC])
        negmax = sb("negmax", [P, 2, QT])
        den = sb("den", [P, 4, QT])
        den_u = sb("den_u", [P, 4, QT])
        den_t = sb("den_t", [P, QT, 4])
        rden = sb("rden", [P, QT, 4])
        mparts = sb("mparts", [P, 2, 3, QT], BF16)
        mres = sb("mres", [P, 2, QT])
        zero8 = sb("zero8", [P, QT])
        mT = sb("mT", [P, P], BF16)
        dmask = sb("dmask", [P, QT])
        identb = sb("identb", [P, P], BF16)
        warm = sb("warm", [P, 2])
        pause = sb("pause", [P, 1])
        causal = sb("causal", [P, P])
        cst0 = sb("cst0", [P, 1])
        router = sb("router", [P, KC, E])
        rt = sb("rt", [P, N])
        po_sb = rt[:, 0:N]
        TE = TPC * E
        lg = rt[:, 0:TE].rearrange("p (t e) -> p t e", e=E)
        top = rt[:, TE:TE + TPC * 8].rearrange("p (t e) -> p t e", e=8)
        topi = rt[:, 2 * TE:2 * TE + TPC * 8].bitcast(U32).rearrange("p (t e) -> p t e", e=8)
        slot_e = rt[:, 3 * TE:4 * TE].rearrange("p (t e) -> p t e", e=E)
        slot_j = rt[:, 4 * TE:6 * TE].rearrange("p (j t e) -> p j t e", j=TOPK, e=E)
        choice = rt[:, 6 * TE:6 * TE + TPC * TOPK].rearrange("p (t j) -> p t j", j=TOPK)
        zero = rt[:, 256:256 + D]
        oh = rt[:, 512:512 + TOPK * TT * E].rearrange("p (j t e) -> p j t e", j=TOPK, e=E)
        oh_bf = sb("oh_bf", [P, TT, E], BF16)
        gate = sb("gate", [P, TOPK, TT])
        gtmp = sb("gtmp", [P, TT])
        iota_e = sb("iota_e", [P, E])
        lower = sb("lower", [P, P], BF16)
        ones = sb("ones", [P, P], BF16)
        thr = sb("thr", [P, TT])
        cnt = sb("cnt", [P, E])
        ntile = sb("ntile", [P, E])
        tle = sb("tle", [P, E, E])
        endt = sb("endt", [P, E])
        base = sb("base", [P, E])
        posf = sb("posf", [P, TOPK, TT])
        posd = sb("posd", [P, TOPK, TT])
        pos_in = sb("pos_in", [P, TOPK, TT], I32)
        pos = sb("pos", [P, TOPK, TT], I32)
        region = sb("region", [P, E])
        padf = sb("padf", [1, E])
        pad = sb("pad", [1, E], I32)
        assert 3 * NT <= 256
        first, valid, rowf = [rt[0:1, i * NT:(i + 1) * NT] for i in range(3)]
        row = sb("row", [1, NT], I32)
        iota_t = sb("iota_t", [1, NT])
        tabf = sb("tabf", [1, NT])
        tab = sb("tab", [1, NT], I32)
        x2T = sb("x2T", [P, KC, CT])
        tmp_e = sb("tmp_e", [P, E, E])
        x2T_f = x2T[:, :, :].rearrange("p k t -> p (k t)")
        tmp = x2T_f[:, 0:TOPK * TT * E].rearrange("p (j t e) -> p j t e", j=TOPK, e=E)
        tmp_t = x2T_f[:, TT * E:2 * TT * E].rearrange("p (e t) -> p e t", e=E)
        tmp_n = x2T_f[0:1, 0:NT * E].rearrange("p (t e) -> p t e", e=E)

        NG = 8
        ym = yx_f if NB == 4 else pa
        o = 0

        def piece(n):
            nonlocal o
            o += n
            return ym[:, o - n:o]

        xslot = [piece(D) for _ in range(2)]
        yslot = [piece(D) for _ in range(2)]
        hid = piece(FF)
        hidT = piece(FF).rearrange("p (c t) -> p c t", c=FC)
        xsT = piece(KC * P).rearrange("p (k t) -> p k t", k=KC)
        ct = [piece(2 * D).rearrange("p (j d) -> p j d", j=2) for _ in range(NG)]

        ps = ctx.enter_context(nc.psum_tensor("ps", [P, 8, 512], F32))

        def bk(i):
            return ps[:, i, :]

        s_w = sem("s_w")
        s_ident = sem("s_ident")
        s_const = sem("s_const")
        s_x = [sem("s_x0"), sem("s_x1")]
        s_bn = sem("s_bn")
        s_var = sem("s_var")
        s_std = sem("s_std")
        s_xn = sem("s_xn")
        s_xt = sem("s_xt")
        s_xta = sem("s_xta")
        s_xtd = sem("s_xtd")
        s_qk = sem("s_qk")
        s_p1 = sem("s_p1")
        s_res = sem("s_res")
        s_p2 = sem("s_p2")
        s_p3 = sem("s_p3")
        s_st = [sem(f"s_st{g}") for g in range(4)]
        s_v = sem("s_v")
        s_ve = sem("s_ve")
        s_wfc = sem("s_wfc")
        s_ld = [sem(f"s_ld{i}") for i in range(4)]
        s_S = sem("s_S")
        s_max = sem("s_max")
        s_exp = sem("s_exp")
        s_denc = sem("s_denc")
        s_sp = sem("s_sp")
        s_mtp = sem("s_mtp")
        s_mtc = sem("s_mtc")
        s_ex = sem("s_ex")
        s_vc = sem("s_vc")
        s_ST = sem("s_ST")
        s_expB = sem("s_expB")
        s_mask = sem("s_mask")
        s_pv = sem("s_pv")
        s_poz = sem("s_poz")
        s_poc = sem("s_poc")
        s_T4 = sem("s_T4")
        s_oc = sem("s_oc")
        s_nc = sem("s_nc")
        s_norm = sem("s_norm")
        s_zero = sem("s_zero")
        s_xsz = sem("s_xsz")
        s_pad = sem("s_pad")
        s_xin = sem("s_xin")
        s_wp = sem("s_wp")
        s_bny = sem("s_bny")
        s_vary = sem("s_vary")
        s_stdy = sem("s_stdy")
        s_bnx = sem("s_bnx")
        s_varx = sem("s_varx")
        s_stdx = sem("s_stdx")
        s_y2 = sem("s_y2")
        s_add = sem("s_add")
        s_x2 = sem("s_x2")
        s_x2t = sem("s_x2t")
        s_x2e = sem("s_x2e")
        s_lg = sem("s_lg")
        s_r = sem("s_r")
        s_d2 = sem("s_d2")
        s_ex2 = sem("s_ex2")
        s_oh = sem("s_oh")
        s_rank = sem("s_rank")
        s_rt = sem("s_rt")
        s_rp = sem("s_rp")
        s_pos = sem("s_pos")
        s_pos2 = sem("s_pos2")
        s_tab = sem("s_tab")
        s_sc = sem("s_sc")
        s_xs = [sem("s_xs0"), sem("s_xs1")]
        s_mt = sem("s_mt")
        s_me = sem("s_me")
        s_fc = sem("s_fc")
        s_ge = sem("s_ge")
        s_ht = sem("s_ht")
        s_hea = sem("s_hea")
        s_hed = sem("s_hed")
        s_pr = sem("s_pr")
        s_yo = sem("s_yo")
        s_ys = [sem("s_ys0"), sem("s_ys1")]
        s_g = [sem(f"s_g{i}") for i in range(NG)]
        s_cf = sem("s_cf")
        s_cb = sem("s_cb")
        s_var3 = sem("s_var3")
        s_std3 = sem("s_std3")
        s_o = sem("s_o")
        s_out = [sem(f"s_out{i}") for i in range(NG)]
        s_warm = sem("s_warm")

        block = ctx.enter_context(nc.Block())

        U = 4 * QT
        NGR = NH // 4
        LAG_M, LAG_E, LAG_B, LAG_P = 9, 10, 12, 14
        STEP_C, STEP_T, STEP_N, TAIL = (10, 13), (12, 16), (12, 16), 19
        STEP_D = 2 * QT + 2
        MROW = 96
        MR = 3 * QT
        assert SROWS == MROW and N == 1024

        chunks = []
        for i in range(QT):
            for q0, q1 in ((i * P, 512), (max(i * P, 512), N)):
                if q0 < q1:
                    chunks.append((i, q0, q1 - q0, len(chunks)))
        NC = len(chunks)
        of_tile = {i: [ch for ch in chunks if ch[0] == i] for i in range(QT)}
        assert NC % NET == 0

        events = []
        for k in range(U):
            if k in STEP_T:
                events.append(("t", k, -4, STEP_T.index(k)))
            if (k - LAG_M) % QT == 0:
                events.append(("m", k, (k - LAG_M) // QT, 0))
            for ch in of_tile[(k - LAG_B) % QT]:
                events.append(("s", k, (k - LAG_B) // QT, ch[3]))
        assert len(events) % 2 == 0
        at_event = {ev: n for n, ev in enumerate(events)}

        def ebank(kind, k, hl, c):
            return 4 + at_event[(kind, k, hl, c)] % 2

        def free_bank(pe, p, first, tail, ev):
            n = at_event[ev] - 2
            while True:
                back, m = (1, n + len(events)) if n < 0 else (0, n)
                kind, _, hl, c = events[m]
                if first and back:
                    return
                if not back and not live(hl, first, tail):
                    n -= 2
                    continue
                h = 4 * p + hl - 4 * back
                if kind == "m":
                    pe.wait_ge(s_mtc, h + 1)
                elif kind == "s":
                    pe.wait_ge(s_expB, NC * h + c + 1)
                else:
                    pe.wait_ge(s_oc, 2 * (p - back - 1) + c + 1)
                return

        CRT, CRP = 5, 3

        def live(u, first, tail):
            return not (first and u < 0) and not (tail and u >= 0)

        def wait_pos(eng, s, v):
            if isinstance(v, int) and v <= 0:
                return
            eng.wait_ge(s, v)

        def groups(eng, body):
            body(0, range(U), True, False)
            with eng.Fori(1, NGR) as p:
                body(p, range(U), False, False)
            body(NGR, range(TAIL), False, True)

        def chunk_steps(eng, step):
            for cc in range(CPB):
                step(0, cc, NB > 1 or cc + 1 < CPB)
            if NB > 2:
                with eng.Fori(1, NB - 1) as b:
                    for cc in range(CPB):
                        step(b, cc, True)
            if NB > 1:
                for cc in range(CPB):
                    step(NB - 1, cc, cc + 1 < CPB)

        @block.sync
        def _(sp):
            for s in range(CPB):
                sp.dma_start(xc[s], x_t[:, s * TPC:(s + 1) * TPC, :]).then_inc(s_x[s], 16)
            for w, src in enumerate((wq_d, wk_d, wv_d)):
                sp.dma_start(wqkv[:, w], src.rearrange("(k p) d -> p k d", p=P)).then_inc(s_w, 16)
            sp.dma_start(router[:, :, :], router_d.rearrange("(k p) e -> p k e", p=P)).then_inc(s_w, 16)

            def store_parts(b, cc):
                c = CPB * b + cc
                for g in range(4):
                    sp.wait_ge(s_p3, 4 * c + g + 1)
                    ty, cg = divmod(g, KC)
                    sp.dma_start(qk_d[ty, :, ds(b * D + cg * P, P), cc * CT:(cc + 1) * CT]
                                 .rearrange("s r t -> r s t"), parts[g]).then_inc(s_st[g], 16)

            def load_next(b, cc):
                sp.wait_ge(s_xt, KC * (CPB * b + cc + 1))
                sp.dma_start(xc[cc], x_t[:, ds((CPB * (b + 1) + cc) * TPC, TPC), :]).then_inc(s_x[cc], 16)

            if NB > 1:
                with sp.Fori(0, NB - 1) as b:
                    for cc in range(CPB):
                        load_next(b, cc)
                        store_parts(b, cc)
            Q_TERMS, K_TERMS = (0, 1, 2, 0, 1, 0), (0, 0, 0, 1, 1, 2)

            def load_head(h, s):
                for ty, (dst, terms) in enumerate(((qs[s], Q_TERMS), (ks[s], K_TERMS))):
                    for r, part in enumerate(terms):
                        sp.dma_start(dst[r * DH:(r + 1) * DH, :], qk_d[ty, part, ds(h * DH, DH), :])\
                          .then_inc(s_ld[s], 16)

            def first_heads():
                sp.wait_ge(s_const, 18)
                for g in range(4):
                    sp.wait_ge(s_st[g], 16 * CPB)
                for hl in range(4):
                    load_head(hl, hl)

            for cc in range(CPB):
                store_parts(NB - 1, cc)
                if cc == (CPB - 1 if NB == 1 else 0):
                    first_heads()
            for g in range(4):
                sp.wait_ge(s_st[g], 16 * NB * CPB)
            sp.wait_ge(s_ve, 2 * NB * CPB)
            sp.dma_start(x1[:, :, :], x_t).then_inc(s_xin, 16)
            wfc_v = wfc_d.rearrange("e (k p) f -> p (e k) f", p=P)
            wfc_s = wfc[:, :].rearrange("p (c f) -> p c f", f=FF)
            PIECES = 2 * E * KC
            HF = FF // 2

            def load_wfc(j):
                at = (slice(None), ds(j // 2, 1), ds((j % 2) * HF, HF))
                sp.dma_start(wfc_s[at], wfc_v[at]).then_inc(s_wfc, 16)

            for j in [0, 1] + list(range(2 * NGR, PIECES)):
                load_wfc(j)
            with sp.Fori(1, NGR) as p:
                for hl in range(4):
                    sp.wait_ge(s_ST, NC * (4 * p + hl - 3))
                    load_head(4 * p + hl, hl)
                    if hl % 2:
                        load_wfc(2 * p + hl // 2)

            sp.wait_ge(s_pv, NH * QT)
            for e in range(E):
                sp.dma_start(arena[:, e * WSTEP:(e + 1) * WSTEP].rearrange("p (c d) -> p c d", c=FC),
                             wproj_d[e].rearrange("(c p) d -> p c d", p=P)).then_inc(s_wp, 16)

            sp.wait_ge(s_pad, 1)
            sp.wait_ge(s_zero, 2)
            with sp.Fori(0, E) as e:
                at = sp.value_load(pad[0:1, ds(e, 1)], min_val=0, max_val=E * REG - P)
                sp.dma_start(xs_d[ds(at, P), :], zero).then_inc(s_xsz, 16)

            def fetch(t, s):
                at = sp.value_load(row[0:1, ds(t, 1)], min_val=0, max_val=E * REG - P)
                sp.dma_start(xslot[s], xs_d[ds(at, P), :]).then_inc(s_xs[s], 16)

            sp.wait_ge(s_tab, 1)
            sp.wait_ge(s_xsz, 16 * E)
            sp.wait_ge(s_sc, 16 * TT * TOPK)
            for s in range(2):
                fetch(s, s)

            def store_tile(t, s):
                sp.wait_ge(s_yo, t + 1)
                sp.dma_start(ys_d[ds(t * P, P), :], yslot[s]).then_inc(s_ys[s], 16)

            def load_tile(t, s):
                sp.wait_ge(s_mt, t - 1)
                fetch(t, s)

            load_tile(2, 0)
            NL = (NT - 3) // 2
            with sp.Fori(0, NL) as q:
                for s in range(2):
                    load_tile(2 * q + 3 + s, 1 - s)
                    store_tile(2 * q + s, s)
            for t in range(2 * NL + 3, NT):
                load_tile(t, t % 2)
            for t in range(2 * NL, NT):
                store_tile(t, t % 2)

            with sp.Fori(0, TT // NG) as g:
                for j in range(NG):
                    sp.wait_ge(s_o, NG * g + j + 1)
                    sp.dma_start(out_t[:, ds(NG * g + j, 1), :], ct[j][:, 1:2, :]).then_inc(s_out[j], 16)
            for j in range(NG):
                sp.wait_ge(s_out[j], 16 * TT // NG)

        @block.gpsimd
        def _(pool):
            pool.memset(ident[:, :], 0.0).then_inc(s_const, 1)
            pool.memset(lower[:, :], 1.0).then_inc(s_const, 1)
            pool.memset(tle[:, :, :], 1.0).then_inc(s_const, 1)
            pool.memset(ones[:, :], 1.0).then_inc(s_const, 1)
            pool.memset(causal[:, :], 1.0).then_inc(s_const, 1)
            pool.memset(identb[:, :], 0.0).then_inc(s_const, 1)
            pool.memset(dmask[:, :], 0.0).then_inc(s_const, 1)
            pool.memset(zero8[:, :], 0.0).then_inc(s_const, 1)
            for s in range(2):
                pool.memset(vh[s], 1.0).then_inc(s_const, 1)
            for s in range(4):
                pool.memset(ks[s], 1.0).then_inc(s_const, 1)
            pool.memset(cst0[:, :], 0.0).then_inc(s_zero, 1)
            pool.iota(iota_e[:, :], [[1, E]], base=0, channel_multiplier=0,
                      allow_small_or_imprecise_dtypes=True).then_inc(s_const, 1)
            pool.iota(region[:, :], [[REG, E]], base=0, channel_multiplier=0,
                      allow_small_or_imprecise_dtypes=True).then_inc(s_const, 1)
            pool.iota(thr[:, :], [[P, TT]], base=0, channel_multiplier=0,
                      allow_small_or_imprecise_dtypes=True).then_inc(s_const, 1)
            pool.iota(iota_t[:, :], [[1, NT]], base=0, channel_multiplier=0,
                      allow_small_or_imprecise_dtypes=True).then_inc(s_const, 1)
            pool.wait_ge(s_const, 18)
            pool.affine_select(out=ident[:, :], in_=ident[:, :], compare_op=ALU.not_equal, fill=1.0,
                               base=0, pattern=[[-1, P]], channel_multiplier=1).then_inc(s_ident, 1)
            pool.affine_select(out=lower[:, :], in_=lower[:, :], compare_op=ALU.is_gt, fill=0.0,
                               base=0, pattern=[[1, P]], channel_multiplier=-1).then_inc(s_const, 1)
            pool.affine_select(out=causal[:, :], in_=causal[:, :], compare_op=ALU.is_ge, fill=0.0, base=0,
                               pattern=[[1, P]], channel_multiplier=-1).then_inc(s_const, 1)
            pool.affine_select(out=identb[:, :], in_=identb[:, :], compare_op=ALU.not_equal, fill=1.0,
                               base=0, pattern=[[-1, P]], channel_multiplier=1).then_inc(s_const, 1)
            for part in range(3):
                if part:
                    pool.wait_ge(s_const, 21 + part)
                pool.affine_select(out=dmask[:, :], in_=dmask[:, :], compare_op=ALU.not_equal, fill=1.0,
                                   base=-MROW - QT * part, pattern=[[-1, QT]],
                                   channel_multiplier=1).then_inc(s_const, 1)
            pool.affine_select(out=tle[:, :, :], in_=tle[:, :, :], compare_op=ALU.is_ge, fill=0.0,
                               base=0, pattern=[[1, E], [-1, E]], channel_multiplier=0).then_inc(s_const, 1)
            def split(b, cc):
                for g in range(4):
                    n = 4 * (CPB * b + cc) + g
                    pool.wait_ge(s_p2, n + 1)
                    pool.tensor_tensor(parts[g][:, 2, :], resid[g % 2], parts[g][:, 1, :],
                                       ALU.subtract).then_inc(s_p3, 1)

            with pool.Fori(0, NB) as b:
                for cc in range(CPB):
                    split(b, cc)

            pool.wait_ge(s_const, 24)

            def body(p, ks_, first, tail):
                for k in ks_:
                    if k % QT == 0 and live(k - QT, first, tail):
                        hl = k // QT - 1
                        h, s = 4 * p + hl, hl % 2
                        nm, parts_ = negmax[:, s, :], mparts[:, s]
                        pool.wait_ge(s_max, QT * h + QT)
                        wait_pos(pool, s_mtp, h - 1)
                        pool.tensor_tensor(parts_[:, 0, :], nm, zero8[:, :], ALU.add).then_inc(s_sp, 1)
                        pool.wait_ge(s_sp, 4 * h + 1)
                        pool.tensor_tensor(mres[:, s, :], nm, parts_[:, 0, :], ALU.subtract).then_inc(s_sp, 1)
                        pool.wait_ge(s_sp, 4 * h + 2)
                        pool.tensor_tensor(parts_[:, 1, :], mres[:, s, :], zero8[:, :], ALU.add).then_inc(s_sp, 1)
                        pool.wait_ge(s_sp, 4 * h + 3)
                        pool.tensor_tensor(parts_[:, 2, :], mres[:, s, :], parts_[:, 1, :],
                                           ALU.subtract).then_inc(s_sp, 1)
                    if (k - LAG_E) % QT == 0 and live(k - LAG_E, first, tail):
                        hl = (k - LAG_E) // QT
                        h = 4 * p + hl
                        wait_pos(pool, s_pv, QT * (h - 1))
                        wait_pos(pool, s_mask, U * p + k - LAG_B)
                        pool.wait_ge(s_mtc, h + 1)
                        pool.tensor_tensor(qs[hl % 4][MROW:MROW + MR, :].rearrange("p (i q) -> p i q", i=QT),
                                           mT[MROW:MROW + MR, :].unsqueeze(1).to_broadcast([MR, QT, P]),
                                           dmask[MROW:MROW + MR, :].unsqueeze(2).to_broadcast([MR, QT, P]),
                                           ALU.mult).then_inc(s_ex, 1)
                        pool.wait_ge(s_ex, h + 1)
                        pool.tensor_copy(vh[hl % 2][:, :, 0:DH], v_sb[:, ds(h * QT * DH, QT * DH)]
                                         .rearrange("p (i d) -> p i d", d=DH)).then_inc(s_vc, 1)
                    if live(k - LAG_B, first, tail):
                        hl, i = divmod(k - LAG_B, QT)
                        h = 4 * p + hl
                        _, _, _, n = of_tile[i][0]
                        pool.wait_ge(s_expB, NC * h + n + 1)
                        blk = et_sb[n % NET][:, 0:P]
                        pool.tensor_tensor(blk, blk, causal[:, :], ALU.mult).then_inc(s_mask, 1)

            groups(pool, body)

            pool.wait_ge(s_xin, 16)
            pool.wait_ge(s_norm, 2 * NGR)
            pool.memset(zero, 0.0).then_inc(s_zero, 1)

            def add_x1(g):
                pool.wait_ge(s_y2, g + 1)
                pool.tensor_tensor(x1[:, g * TPC:(g + 1) * TPC, :], x1[:, g * TPC:(g + 1) * TPC, :],
                                   yx[:, g * TPC:(g + 1) * TPC, :], ALU.add).then_inc(s_add, 1)

            def scatter(g):
                pool.wait_ge(s_x2, g + 1)
                pool.wait_ge(s_pos, g + 1)
                for t in range(g * TPC, (g + 1) * TPC):
                    for j in range(TOPK):
                        pool.indirect_dma_start(out=xs_d, in_=yx[:, t, :], in_offset=None,
                                                out_offset=bass.IndirectOffsetOnAxis(ap=pos_in[:, j, t:t + 1], axis=0))\
                            .then_inc(s_sc, 16)

            G = TT // TPC
            for g in range(G + 3):
                if g < G:
                    add_x1(g)
                if g >= 3:
                    scatter(g - 3)
            pool.wait_ge(s_pos2, 1)

            for s in range(2):
                pool.wait_ge(s_ys[s], 16 * ((NT + 1 - s) // 2))
            for t in range(TT):
                if t >= NG:
                    pool.wait_ge(s_o, t - NG + 1)
                    pool.wait_ge(s_out[t % NG], 16 * (t // NG))
                for j in range(TOPK):
                    pool.indirect_dma_start(out=ct[t % NG][:, j, :], out_offset=None, in_=ys_d,
                                            in_offset=bass.IndirectOffsetOnAxis(ap=pos[:, j, t:t + 1], axis=0))\
                        .then_inc(s_g[t % NG], 16)

        @block.scalar
        def _(act):
            act.wait_ge(s_zero, 1)
            nc.scalar.activation(warm[:, 0:1], cst0[:, 0:1], ACT.Sqrt).then_inc(s_warm, 1)

            def root_c(n, s):
                act.wait_ge(s_var, n + 1)
                nc.scalar.activation(std[:, s, :], mv[:, s, :, 1], ACT.Sqrt).then_inc(s_std, 1)

            def copy_xn(n, s):
                act.wait_ge(s_xt, KC * n + 1)
                wait_pos(act, s_v, 2 * (n - 1))
                nc.scalar.copy(xnT[s][:, 0, :], bk(0)).then_inc(s_xta, 1)

            def project(b, cc, nxt):
                c = CPB * b + cc
                for g in range(4):
                    if nxt and g == 2:
                        root_c(c + 1, 1 - cc)
                    act.wait_ge(s_qk, 4 * c + g + 1)
                    wait_pos(act, s_st[g], 16 * c)
                    nc.scalar.mul(parts[g][:, 0, :], bk(2 + g), Q_SCALE if g < KC else 1.0).then_inc(s_p1, 1)
                if nxt:
                    copy_xn(c + 1, 1 - cc)
                for j in range(2):
                    act.wait_ge(s_v, 2 * c + j + 1)
                    for t in range(2):
                        i = TPC * cc + 2 * j + t
                        dst = v_sb.rearrange("p (b h i d) -> p b h i d", b=NB, h=H, i=QT)[:, ds(b, 1), :, i, :]
                        ins = nc.scalar.copy(dst, bk(6 + j)[:, t * D:(t + 1) * D]
                                             .rearrange("p (b h d) -> p b h d", b=1, h=H))
                    ins.then_inc(s_ve, 1)

            root_c(0, 0)
            copy_xn(0, 0)
            chunk_steps(act, project)
            act.wait_ge(s_warm, 1)
            nc.scalar.activation(warm[:, 1:2], cst0[:, 0:1], ACT.Exp).then_inc(s_warm, 1)

            def body(p, ks_, first, tail):
                for k in ks_:
                    if (k - LAG_M) % QT == 0 and live(k - LAG_M, first, tail):
                        hl = (k - LAG_M) // QT
                        h = 4 * p + hl
                        act.wait_ge(s_mtp, h + 1)
                        wait_pos(act, s_ex, h)
                        nc.scalar.copy(mT[MROW:MROW + MR, :],
                                       bk(ebank("m", k, hl, 0))[MROW:MROW + MR, 0:P]).then_inc(s_mtc, 1)
                    if live(k - LAG_B, first, tail):
                        hl, i = divmod(k - LAG_B, QT)
                        h = 4 * p + hl
                        for (_, q0, nq, n) in of_tile[i]:
                            act.wait_ge(s_ST, NC * h + n + 1)
                            hb, nb = divmod(n - NET, NC)
                            wait_pos(act, s_pv, QT * (h + hb) + chunks[nb][0] + 1)
                            nc.scalar.activation(et_sb[n % NET][:, 0:nq], bk(ebank("s", k, hl, n))[:, 0:nq],
                                                 ACT.Exp).then_inc(s_expB, 1)
                    if not tail:
                        hl, i = divmod(k, QT)
                        act.wait_ge(s_max, U * p + k + 1)
                        if i == 0:
                            wait_pos(act, s_denc, 4 * p + hl - 3)
                        sc = ps[:, 2 * (k % 2):2 * (k % 2) + 2, :].rearrange("p b q -> p (b q)")[:, i * P:N]
                        nc.scalar.activation(sc, sc, ACT.Exp, bias=negmax[:, hl % 2, i:i + 1],
                                             accum_out=den[:, hl, i:i + 1]).then_inc(s_exp, 1)

            groups(act, body)

            act.wait_ge(s_warm, 2)
            nc.scalar.activation(warm[:, 0:1], cst0[:, 0:1], ACT.Sqrt).then_inc(s_warm, 1)
            def root_y(g):
                act.wait_ge(s_vary, g + 1)
                nc.scalar.activation(std[:, 0, :], mv[:, 0, :, 1], ACT.Sqrt).then_inc(s_stdy, 1)

            def root_x(g):
                act.wait_ge(s_varx, g + 1)
                nc.scalar.activation(std[:, 1, :], mv[:, 1, :, 1], ACT.Sqrt).then_inc(s_stdx, 1)

            def copy_x2(g):
                for kc in range(KC):
                    act.wait_ge(s_x2t, KC * g + kc + 1)
                    nc.scalar.copy(x2T[:, kc, :], bk(kc)).then_inc(s_x2e, 1)

            G = TT // TPC
            root_y(0)
            root_y(1)
            root_x(0)
            if G > 2:
                with act.Fori(2, G) as g:
                    root_y(g)
                    root_x(g - 1)
                    copy_x2(g - 2)
            root_x(G - 1)
            copy_x2(G - 2)
            copy_x2(G - 1)
            act.wait_ge(s_warm, 3)
            act.wait_ge(s_d2, TT // TPC)
            nc.scalar.activation(gtmp[:, :], gtmp[:, :], ACT.Exp).then_inc(s_ex2, 1)
            nc.scalar.activation(warm[:, 1:2], cst0[:, 0:1], ACT.Gelu).then_inc(s_warm, 1)

            def mix(t):
                for hf in range(2):
                    act.wait_ge(s_fc, 2 * t + hf + 1)
                    wait_pos(act, s_ht, 2 * t)
                    nc.scalar.activation(hid[:, hf * 512:(hf + 1) * 512], bk(1 + hf), ACT.Gelu).then_inc(s_ge, 1)
                act.wait_ge(s_ht, 2 * t + 1)
                wait_pos(act, s_pr, t)
                nc.scalar.copy(hidT[:, 0:4, :], bk(3).rearrange("p (c t) -> p c t", c=4)).then_inc(s_hea, 1)

            mix(0)
            with act.Fori(1, NT) as t:
                mix(t)

            act.wait_ge(s_warm, 4)
            nc.scalar.activation(warm[:, 0:1], cst0[:, 0:1], ACT.Sqrt).then_inc(s_warm, 1)
            with act.Fori(0, TT // 2) as q:
                for s in range(2):
                    act.wait_ge(s_var3, 2 * q + s + 1)
                    nc.scalar.activation(std[:, s, 0:1], mv[:, s, 0, 1:2], ACT.Sqrt).then_inc(s_std3, 1)
            act.wait_ge(s_warm, 5)

        @block.tensor
        def _(pe):
            pe.wait_ge(s_ident, 1)
            pe.wait_ge(s_w, 64)

            def turn(n, s):
                pe.wait_ge(s_xn, n + 1)
                for kc in range(KC):
                    wait_pos(pe, (s_xta, s_xtd)[kc], n)
                    for t in range(TPC):
                        ins = nc.tensor.transpose(bk(kc)[:, t * P:(t + 1) * P], xc[s][:, t, kc * P:(kc + 1) * P],
                                                  ident[:, :])
                    ins.then_inc(s_xt, 1)

            def project(b, cc, nxt):
                c = CPB * b + cc
                pe.wait_ge(s_xta, c + 1)
                pe.wait_ge(s_xtd, c + 1)
                for g in range(4):
                    wait_pos(pe, s_res, 4 * c + g - 3)
                    ty, cg = divmod(g, KC)
                    for kc in range(KC):
                        ins = nc.tensor.matmul(bk(2 + g), wqkv[:, ty, kc, cg * P:(cg + 1) * P], xnT[cc][:, kc, :],
                                               start=(kc == 0), stop=(kc == KC - 1))
                    ins.then_inc(s_qk, 1)
                if nxt:
                    turn(c + 1, 1 - cc)
                for j in range(2):
                    wait_pos(pe, s_ve, 2 * c + j - 1)
                    for t in range(2):
                        for kc in range(KC):
                            ins = nc.tensor.matmul(bk(6 + j)[:, t * D:(t + 1) * D],
                                                   xnT[cc][:, kc, (2 * j + t) * P:(2 * j + t + 1) * P],
                                                   wqkv[:, 2, kc, :], start=(kc == 0), stop=(kc == KC - 1))
                    ins.then_inc(s_v, 1)

            turn(0, 0)
            chunk_steps(pe, project)
            pe.wait_ge(s_res, 4 * NB * CPB)
            pe.wait_ge(s_ve, 2 * NB * CPB)

            def body(p, ks_, first, tail):
                for k in ks_:
                    if k in STEP_T and not first:
                        b = STEP_T.index(k)
                        ev = ("t", k, -4, b)
                        free_bank(pe, p, first, tail, ev)
                        pe.wait_ge(s_poc, 2 * p - 1 + b)
                        for t in range(4):
                            ins = nc.tensor.transpose(bk(ebank(*ev))[:, t * P:(t + 1) * P],
                                                      po_sb[:, (4 * b + t) * P:(4 * b + t + 1) * P], ident[:, :])
                        ins.then_inc(s_T4, 1)
                    if not tail:
                        hl, i = divmod(k, QT)
                        if i == 0:
                            pe.wait_ge(s_ld[hl], 16 * 2 * TERMS * (p + 1))
                        wait_pos(pe, s_exp, U * p + k - 1)
                        for hf in range(2):
                            ins = nc.tensor.matmul(bk(2 * (k % 2) + hf), qs[hl][0:SROWS, i * P:(i + 1) * P],
                                                   ks[hl][0:SROWS, hf * 512:(hf + 1) * 512], start=True, stop=True)
                        ins.then_inc(s_S, 1)
                    if (k - LAG_M) % QT == 0 and live(k - LAG_M, first, tail):
                        hl = (k - LAG_M) // QT
                        h = 4 * p + hl
                        free_bank(pe, p, first, tail, ("m", k, hl, 0))
                        pe.wait_ge(s_sp, 4 * h + 4)
                        nc.tensor.matmul(bk(ebank("m", k, hl, 0))[MROW:MROW + MR, 0:P],
                                         mparts[:, hl % 2].rearrange("p s i -> p (s i)"), identb[:, :],
                                         start=True, stop=True).then_inc(s_mtp, 1)
                    if live(k - LAG_B, first, tail):
                        hl, i = divmod(k - LAG_B, QT)
                        h = 4 * p + hl
                        if i == 0:
                            pe.wait_ge(s_ex, h + 1)
                        for (_, q0, nq, n) in of_tile[i]:
                            free_bank(pe, p, first, tail, ("s", k, hl, n))
                            nc.tensor.matmul(bk(ebank("s", k, hl, n))[:, 0:nq],
                                             ks[hl % 4][0:MROW + MR, i * P:(i + 1) * P],
                                             qs[hl % 4][0:MROW + MR, q0:q0 + nq],
                                             start=True, stop=True).then_inc(s_ST, 1)
                    if live(k - LAG_P, first, tail):
                        hl, i = divmod(k - LAG_P, QT)
                        h, j = 4 * p + hl, 32 * (hl % 4)
                        if i == 0:
                            pe.wait_ge(s_vc, h + 1)
                        for (_, q0, nq, n) in of_tile[i]:
                            pe.wait_ge(s_expB, NC * h + n + 1)
                            out, et = bk(6 + q0 // 512), et_sb[n % NET]
                            if i == 0 and hl == 0:
                                wait_pos(pe, s_poc, 2 * p - 1 + q0 // 512)
                            q = q0 % 512
                            diag = P if q0 == i * P else 0
                            if nq > diag:
                                ins = nc.tensor.matmul(out[j:j + VW, q + diag:q + nq], vh[hl % 2][:, i, :],
                                                       et[:, diag:nq], start=(i == 0), stop=False,
                                                       skip_group_check=True)
                            if diag:
                                pe.wait_ge(s_mask, QT * h + i + 1)
                                ins = nc.tensor.matmul(out[j:j + DH, q:q + P], vh[hl % 2][:, i, 0:DH], et[:, 0:P],
                                                       start=False, stop=False, skip_group_check=True)
                        ins.then_inc(s_pv, 1)

            pe.wait_ge(s_poz, 1)
            pe.wait_ge(s_const, 24)
            groups(pe, body)

            pe.wait_ge(s_expB, NC * NH)
            pe.wait_ge(s_exp, QT * NH)
            pe.wait_ge(s_norm, 2 * NGR)

            def route(g):
                pe.wait_ge(s_x2, g + 1)
                for kc in range(KC):
                    wait_pos(pe, s_x2e, KC * g + kc - 1)
                    for t in range(TPC):
                        ins = nc.tensor.transpose(bk(kc)[:, t * P:(t + 1) * P],
                                                  yx[:, g * TPC + t, kc * P:(kc + 1) * P], ident[:, :])
                    ins.then_inc(s_x2t, 1)
                pe.wait_ge(s_x2e, KC * (g + 1))
                for t in range(TPC):
                    for kc in range(KC):
                        ins = nc.tensor.matmul(bk(2)[:, (g * TPC + t) * E:(g * TPC + t + 1) * E],
                                               x2T[:, kc, t * P:(t + 1) * P], router[:, kc, :],
                                               start=(kc == 0), stop=(kc == KC - 1))
                ins.then_inc(s_lg, 1)

            rank = bk(3)[:, 0:(TT + 1) * E].rearrange("p (t e) -> p t e", e=E)

            def count(g):
                pe.wait_ge(s_oh, g + 1)
                wait_pos(pe, s_rp, CRP * (g - 1) + 1 if g else 0)
                nc.tensor.matmul(rank[:, g * TPC:(g + 1) * TPC, :], lower[:, :], oh_bf[:, g * TPC:(g + 1) * TPC, :],
                                 start=(g == 0), stop=False, skip_group_check=True)
                for t in range(g * TPC, (g + 1) * TPC):
                    ins = nc.tensor.matmul(rank[:, t + 1:TT + 1, :], ones[:, :],
                                           oh_bf[:, t, :].unsqueeze(1).to_broadcast([P, TT - t, E]),
                                           start=False, stop=(t == TT - 1), skip_group_check=True)
                ins.then_inc(s_rank, 1)

            G = TT // TPC
            route(0)
            for g in range(1, G):
                count(g - 1)
                route(g)
            count(G - 1)

            pe.wait_ge(s_tab, 1)
            pe.wait_ge(s_wfc, 16 * 2 * E * KC)

            def transpose_x(t, s):
                pe.wait_ge(s_xs[s], 16 * (t // 2 + 1) if isinstance(t, int) else t * 8 + 8 * (2 - s))
                wait_pos(pe, s_me, t)
                for kc in range(KC):
                    ins = nc.tensor.transpose(bk(0)[:, kc * P:(kc + 1) * P], xslot[s][:, kc * P:(kc + 1) * P],
                                              ident[:, :])
                ins.then_inc(s_mt, 1)

            def first_product(t, off):
                pe.wait_ge(s_me, t + 1)
                for hf in range(2):
                    wait_pos(pe, s_ge, 2 * t + hf - 1)
                    for kc in range(KC):
                        ins = nc.tensor.matmul(bk(1 + hf), xsT[:, kc, :],
                                               wfc[:, ds(off + (kc * FF + hf * 512), 512)],
                                               start=(kc == 0), stop=(kc == KC - 1))
                    ins.then_inc(s_fc, 1)

            def transpose_h(t):
                for hf in range(2):
                    pe.wait_ge(s_ge, 2 * t + hf + 1)
                    wait_pos(pe, (s_hea, s_hed)[hf], t)
                    for c in range(4):
                        ins = nc.tensor.transpose(bk(3 + hf)[:, c * P:(c + 1) * P],
                                                  hid[:, (4 * hf + c) * P:(4 * hf + c + 1) * P], ident[:, :])
                    ins.then_inc(s_ht, 1)

            def second_product(t, s, off):
                wait_pos(pe, s_yo, t - 1)
                pe.wait_ge(s_hea, t + 1)
                for c in range(FC):
                    if c == FC // 2:
                        pe.wait_ge(s_hed, t + 1)
                    ins = nc.tensor.matmul(bk(5 + s)[:, 0:D], hidT[:, c, :], arena[:, ds(off + c * D, D)],
                                           start=(c == 0), stop=(c == FC - 1))
                ins.then_inc(s_pr, 1)

            def expert(t):
                return pe.value_load(tab[0:1, ds(t, 1)], min_val=0, max_val=(E - 1) * WSTEP)

            def step(t, s, first=False, last=False):
                if not first:
                    transpose_h(t - 1)
                if not last:
                    first_product(t, expert(t))
                    if not (isinstance(t, int) and t == NT - 1):
                        transpose_x(t + 1, 1 - s)
                if not first:
                    second_product(t - 1, 1 - s, expert(t - 1))

            transpose_x(0, 0)
            step(0, 0, first=True)
            pe.wait_ge(s_wp, 16 * E)
            step(1, 1)
            step(2, 0)
            NL2 = (NT - 4) // 2
            with pe.Fori(0, NL2) as q:
                step(2 * q + 3, 1)
                step(2 * q + 4, 0)
            for t in range(2 * NL2 + 3, NT):
                step(t, t % 2)
            step(NT, NT % 2, last=True)

        @block.vector
        def _(dve):
            def ln_stats(src, s, n, s_chain, chain0, s_out_):
                for t in range(n):
                    nc.vector.bn_stats(stats[:, s, t, :], src[t]).then_inc(s_chain, 1)
                dve.wait_ge(s_chain, chain0 + n)
                nc.vector.memset(pause[:, :], 0.0)
                for t in range(n):
                    nc.vector.bn_aggr(mv[:, s, t, :], stats[:, s, t, :]).then_inc(s_chain, 1)
                dve.wait_ge(s_chain, chain0 + 2 * n)
                nc.vector.tensor_scalar(mv[:, s, 0:n, 1], mv[:, s, 0:n, 1], EPS, None, ALU.add).then_inc(s_out_, 1)

            def ln_apply(dst, src, s, n, s_chain, chain1):
                nc.vector.reciprocal(rstd[:, s, 0:n], std[:, s, 0:n]).then_inc(s_chain, 1)
                dve.wait_ge(s_chain, chain1)
                for t in range(n):
                    ins = nc.vector.tensor_scalar(dst[t], src[t], mv[:, s, t, 0:1], rstd[:, s, t:t + 1],
                                                  ALU.subtract, ALU.mult)
                return ins

            CH = 2 * TPC + 1

            def stats_c(n, s, have):
                dve.wait_ge(s_x[s], have)
                ln_stats([xc[s][:, t, :] for t in range(TPC)], s, TPC, s_bn, CH * n, s_var)

            def apply_c(n, s):
                rows = [xc[s][:, t, :] for t in range(TPC)]
                dve.wait_ge(s_std, n + 1)
                ln_apply(rows, rows, s, TPC, s_bn, CH * (n + 1)).then_inc(s_xn, 1)

            def copy_xn(n, s):
                dve.wait_ge(s_xt, KC * (n + 1))
                wait_pos(dve, s_v, 2 * (n - 1))
                nc.vector.tensor_copy(xnT[s][:, 1, :], bk(1)).then_inc(s_xtd, 1)

            def project(b, cc, nxt):
                c = CPB * b + cc
                for g in range(4):
                    if nxt and g == 0:
                        stats_c(c + 1, 1 - cc, 16 * (b + 1 + cc))
                    if nxt and g == 2:
                        apply_c(c + 1, 1 - cc)
                    dve.wait_ge(s_p1, 4 * c + g + 1)
                    wait_pos(dve, s_p3, 4 * c + g - 1)
                    nc.vector.scalar_tensor_tensor(out=resid[g % 2], in0=bk(2 + g),
                                                   scalar=Q_SCALE if g < KC else 1.0, in1=parts[g][:, 0, :],
                                                   op0=ALU.mult, op1=ALU.subtract).then_inc(s_res, 1)
                    dve.wait_ge(s_res, 4 * c + g + 1)
                    wait_pos(dve, s_st[g], 16 * c)
                    nc.vector.tensor_copy(parts[g][:, 1, :], resid[g % 2]).then_inc(s_p2, 1)
                if nxt:
                    copy_xn(c + 1, 1 - cc)

            stats_c(0, 0, 16)
            apply_c(0, 0)
            copy_xn(0, 0)
            chunk_steps(dve, project)

            dve.wait_ge(s_ve, 2 * NB * CPB)
            nc.vector.memset(ps[:, 6:8, :], 0.0).then_inc(s_poz, 1)

            def body(p, ks_, first, tail):
                for k in ks_:
                    if k in STEP_T and not first:
                        b = STEP_T.index(k)
                        dve.wait_ge(s_T4, 2 * p - 1 + b)
                        nc.vector.tensor_copy(po_sb[:, b * 512:(b + 1) * 512],
                                              bk(ebank("t", k, -4, b))).then_inc(s_oc, 1)
                    if not tail:
                        hl, i = divmod(k, QT)
                        dve.wait_ge(s_S, U * p + k + 1)
                        if i == 0:
                            wait_pos(dve, s_sp, 4 * (4 * p + hl - 1))
                        nc.vector.tensor_reduce(negmax[:, hl % 2, i:i + 1], ps[:, 2 * (k % 2):2 * (k % 2) + 2, :],
                                                AX.XY, ALU.max, negate=True).then_inc(s_max, 1)
                    for b in range(2):
                        o4 = po_sb[:, b * 512:(b + 1) * 512].rearrange("p (i h r) -> p i h r", i=4, h=4)
                        sl = slice(4 * b, 4 * b + 4)
                        if first or not STEP_N[b] <= k <= STEP_N[b] + 2:
                            continue
                        if k == STEP_N[b]:
                            dve.wait_ge(s_denc, 4 * p)
                            dve.wait_ge(s_oc, 2 * p - 1 + b)
                            nc.vector.tensor_tensor(den_t[:, sl, :], o4[:, :, :, DH],
                                                    den_u[:, :, sl].rearrange("p h i -> p i h"),
                                                    ALU.add).then_inc(s_nc, 1)
                        elif k == STEP_N[b] + 1:
                            dve.wait_ge(s_nc, 4 * p - 3 + 2 * b)
                            nc.vector.reciprocal(rden[:, sl, :], den_t[:, sl, :]).then_inc(s_nc, 1)
                        else:
                            dve.wait_ge(s_nc, 4 * p - 2 + 2 * b)
                            hh, bb = (4 * (p - 1)) % H, (4 * (p - 1)) // H
                            dst = yx[:, ds(bb * QT + 4 * b, 4), ds(hh * DH, 4 * DH)]
                            nc.vector.tensor_tensor(dst.rearrange("p i (h d) -> p i h d", h=4), o4[:, :, :, 0:DH],
                                                    rden[:, sl, :].unsqueeze(3).to_broadcast([P, 4, 4, DH]),
                                                    ALU.mult).then_inc(s_norm, 1)
                    if k in STEP_C and not first:
                        b = STEP_C.index(k)
                        dve.wait_ge(s_pv, U * p - 4 * (1 - b))
                        nc.vector.tensor_copy(po_sb[:, b * 512:(b + 1) * 512], bk(6 + b)).then_inc(s_poc, 1)
                    if (k - STEP_D) % QT == 0 and live(k - STEP_D, first, tail):
                        hl = (k - STEP_D) // QT
                        dve.wait_ge(s_exp, QT * (4 * p + hl + 1))
                        nc.vector.tensor_copy(den_u[:, hl % 4, :], den[:, hl % 4, :]).then_inc(s_denc, 1)

            groups(dve, body)
            dve.wait_ge(s_norm, 2 * NGR)

            dve.wait_ge(s_xin, 16)
            G = TT // TPC

            def rows(buf, g):
                return [buf[:, ds(g * TPC + t, 1), :] for t in range(TPC)]

            def stats_y(g):
                ln_stats(rows(yx, g), 0, TPC, s_bny, CH * g, s_vary)

            def apply_y(g):
                dve.wait_ge(s_stdy, g + 1)
                ln_apply(rows(yx, g), rows(yx, g), 0, TPC, s_bny, CH * (g + 1)).then_inc(s_y2, 1)

            def stats_x(g):
                dve.wait_ge(s_add, g + 1)
                ln_stats(rows(x1, g), 1, TPC, s_bnx, CH * g, s_varx)

            def apply_x(g):
                dve.wait_ge(s_stdx, g + 1)
                ln_apply(rows(yx, g), rows(x1, g), 1, TPC, s_bnx, CH * (g + 1)).then_inc(s_x2, 1)

            rank = bk(3)[:, 0:(TT + 1) * E].rearrange("p (t e) -> p t e", e=E)

            def choose(g):
                tiles, n = ds(g * TPC, TPC), CRT * g
                dve.wait_ge(s_lg, g + 1)
                nc.vector.tensor_copy(lg, bk(2)[:, ds(g * TE, TE)].rearrange("p (t e) -> p t e", e=E)).then_inc(s_rt, 1)
                dve.wait_ge(s_rt, n + 1)
                nc.vector.memset(pause[:, :], 0.0)
                for t in range(TPC):
                    ins = nc.vector.max(top[:, t, :], lg[:, t, :])
                ins.then_inc(s_rt, 1)
                dve.wait_ge(s_rt, n + 2)
                nc.vector.memset(pause[:, :], 0.0)
                for t in range(TPC):
                    ins = nc.vector.max_index(topi[:, t, :], top[:, t, :], lg[:, t, :])
                ins.then_inc(s_rt, 1)
                nc.vector.tensor_tensor(gtmp[:, tiles], top[:, :, 1], top[:, :, 0], ALU.subtract).then_inc(s_d2, 1)
                dve.wait_ge(s_rt, n + 3)
                nc.vector.tensor_copy(choice, topi[:, :, 0:TOPK]).then_inc(s_rt, 1)
                dve.wait_ge(s_rt, n + 4)
                for j in range(TOPK):
                    ins = nc.vector.tensor_tensor(oh[:, j, tiles, :],
                                                  choice[:, :, j].unsqueeze(2).to_broadcast([P, TPC, E]),
                                                  iota_e[:, :].unsqueeze(1).to_broadcast([P, TPC, E]), ALU.is_equal)
                ins.then_inc(s_rt, 1)
                dve.wait_ge(s_rt, n + 5)
                nc.vector.tensor_tensor(oh_bf[:, tiles, :], oh[:, 0, tiles, :], oh[:, 1, tiles, :],
                                        ALU.add).then_inc(s_oh, 1)

            def place(g):
                tiles, n = ds(g * TPC, TPC), CRP * g
                dve.wait_ge(s_rank, g + 1)
                nc.vector.tensor_tensor(slot_e, rank[:, tiles, :], region[:, :].unsqueeze(1).to_broadcast([P, TPC, E]),
                                        ALU.add).then_inc(s_rp, 1)
                dve.wait_ge(s_rp, n + 1)
                for j in range(TOPK):
                    ins = nc.vector.tensor_tensor(slot_j[:, j], oh[:, j, tiles, :], slot_e, ALU.mult)
                ins.then_inc(s_rp, 1)
                dve.wait_ge(s_rp, n + 2)
                for j in range(TOPK):
                    ins = nc.vector.tensor_reduce(posf[:, j, tiles], slot_j[:, j], AX.X, ALU.add)
                ins.then_inc(s_rp, 1)
                dve.wait_ge(s_rp, n + 3)
                nc.vector.tensor_copy(pos_in[:, :, tiles], posf[:, :, tiles]).then_inc(s_pos, 1)

            def group(g, third, fourth):
                stats_y(g)
                stats_x(g - 1)
                apply_y(g)
                apply_x(g - 1)
                if third:
                    choose(g - 2)
                if fourth:
                    place(g - 3)

            dve.wait_ge(s_const, 24)
            stats_y(0)
            apply_y(0)
            for g in range(1, min(G, 3)):
                group(g, g >= 2, False)
            if G > 3:
                with dve.Fori(3, G) as g:
                    group(g, True, True)
            stats_x(G - 1)
            apply_x(G - 1)
            if G > 2:
                place(G - 3)
            choose(G - 2)
            choose(G - 1)
            place(G - 2)

            n_r = [0]

            def link(ins):
                n_r[0] += 1
                ins.then_inc(s_r, 1)
                dve.wait_ge(s_r, n_r[0])

            dve.wait_ge(s_rank, G)
            link(nc.vector.tensor_copy(cnt[:, :], rank[:, TT, :]))
            link(nc.vector.tensor_tensor(padf[:, :], cnt[0:1, :], region[0:1, :], ALU.add))
            nc.vector.tensor_copy(pad[:, :], padf[:, :]).then_inc(s_pad, 1)
            place(G - 1)
            dve.wait_ge(s_ex2, 1)
            link(nc.vector.tensor_scalar(gate[:, 1, :], gtmp[:, :], 1.0, None, ALU.add))
            link(nc.vector.reciprocal(gate[:, 0, :], gate[:, 1, :]))
            link(nc.vector.tensor_tensor(gate[:, 1, :], gate[:, 0, :], gtmp[:, :], ALU.mult))
            link(nc.vector.tensor_tensor(tmp_t[:, :, :], cnt[:, :].unsqueeze(2).to_broadcast([P, E, TT]),
                                         thr[:, :].unsqueeze(1).to_broadcast([P, E, TT]), ALU.is_gt))
            link(nc.vector.tensor_reduce(ntile[:, :], tmp_t[:, :, :], AX.X, ALU.add))
            link(nc.vector.tensor_tensor(tmp_e[:, :, :], tle[:, :, :], ntile[:, :].unsqueeze(1).to_broadcast([P, E, E]),
                                         ALU.mult))
            link(nc.vector.tensor_reduce(endt[:, :], tmp_e[:, :, :], AX.X, ALU.add))
            link(nc.vector.tensor_tensor(base[:, :], endt[:, :], ntile[:, :], ALU.subtract))
            link(nc.vector.tensor_tensor(tmp_n[:, :, :], endt[0:1, :].unsqueeze(1).to_broadcast([1, NT, E]),
                                         iota_t[:, :].unsqueeze(2).to_broadcast([1, NT, E]), ALU.is_le))
            link(nc.vector.tensor_reduce(tabf[:, :], tmp_n[:, :, :], AX.X, ALU.add))
            link(nc.vector.tensor_tensor(tmp_n[:, :, :], tmp_n[:, :, :],
                                         ntile[0:1, :].unsqueeze(1).to_broadcast([1, NT, E]), ALU.mult))
            link(nc.vector.tensor_reduce(first[:, :], tmp_n[:, :, :], AX.X, ALU.add))
            link(nc.vector.tensor_scalar(valid[:, :], tabf[:, :], float(E), float(P), ALU.is_lt, ALU.mult))
            link(nc.vector.tensor_tensor(rowf[:, :], iota_t[:, :], first[:, :], ALU.subtract))
            link(nc.vector.tensor_tensor(rowf[:, :], rowf[:, :], valid[:, :], ALU.mult))
            link(nc.vector.tensor_scalar(tabf[:, :], tabf[:, :], float(E - 1), None, ALU.min))
            link(nc.vector.tensor_scalar(first[:, :], tabf[:, :], float(REG), None, ALU.mult))
            link(nc.vector.tensor_tensor(rowf[:, :], rowf[:, :], first[:, :], ALU.add))
            link(nc.vector.tensor_copy(row[:, :], rowf[:, :]))
            link(nc.vector.tensor_scalar(tabf[:, :], tabf[:, :], float(WSTEP), None, ALU.mult))
            nc.vector.tensor_copy(tab[:, :], tabf[:, :]).then_inc(s_tab, 1)
            link(nc.vector.tensor_scalar(base[:, :], base[:, :], float(P), None, ALU.mult))
            link(nc.vector.tensor_tensor(base[:, :], base[:, :], region[:, :], ALU.subtract))
            for j in range(TOPK):
                ins = nc.vector.tensor_tensor(tmp[:, j], oh[:, j], base[:, :].unsqueeze(1).to_broadcast([P, TT, E]),
                                              ALU.mult)
            link(ins)
            for j in range(TOPK):
                ins = nc.vector.tensor_reduce(posd[:, j, :], tmp[:, j], AX.X, ALU.add)
            link(ins)
            link(nc.vector.tensor_tensor(posd[:, :, :], posd[:, :, :], posf[:, :, :], ALU.add))
            nc.vector.tensor_copy(pos[:, :, :], posd[:, :, :]).then_inc(s_pos2, 1)

            def copy_x(t):
                dve.wait_ge(s_mt, t + 1)
                wait_pos(dve, s_fc, 2 * t)
                nc.vector.tensor_copy(xsT[:, :, :], bk(0)[:, 0:KC * P].rearrange("p (k t) -> p k t", k=KC))\
                  .then_inc(s_me, 1)

            def copy_h(t):
                dve.wait_ge(s_ht, 2 * t + 2)
                wait_pos(dve, s_pr, t)
                nc.vector.tensor_copy(hidT[:, 4:8, :], bk(4).rearrange("p (c t) -> p c t", c=4)).then_inc(s_hed, 1)

            def copy_y(t, s):
                dve.wait_ge(s_pr, t + 1)
                if not isinstance(t, int) or t >= 2:
                    dve.wait_ge(s_ys[s], 16 * (t // 2) if isinstance(t, int) else 8 * t - 8 * s)
                nc.vector.tensor_copy(yslot[s], bk(5 + s)[:, 0:D]).then_inc(s_yo, 1)

            def mix(t, s):
                if not isinstance(t, int) or t >= 1:
                    copy_h(t - 1)
                if not isinstance(t, int) or t < NT - 1:
                    copy_x(t + 1)
                if not isinstance(t, int) or t >= 1:
                    copy_y(t - 1, 1 - s)

            copy_x(0)
            mix(0, 0)
            mix(1, 1)
            mix(2, 0)
            NL3 = (NT - 4) // 2
            with dve.Fori(0, NL3) as q:
                mix(2 * q + 3, 1)
                mix(2 * q + 4, 0)
            for t in range(2 * NL3 + 3, NT + 1):
                mix(t, t % 2)

            def combine(t, j, front, back):
                jn, f, b = (j + 1) % NG, (j + 1) % 2, j % 2
                y0, y1 = ct[jn][:, 0:1, :], ct[jn][:, 1:2, :]
                z0, z1 = ct[j][:, 0:1, :], ct[j][:, 1:2, :]
                tn = t + 1
                if front:
                    dve.wait_ge(s_g[jn], 32 * (tn // NG + 1) if isinstance(t, int) else
                                (32 // NG) * (tn - jn) + 32)
                    nc.vector.tensor_scalar(y0, y0, gate[:, 0, ds(tn, 1)], None, ALU.mult).then_inc(s_cf, 1)
                if back:
                    dve.wait_ge(s_std3, t + 1)
                    nc.vector.reciprocal(rstd[:, b, 0:1], std[:, b, 0:1]).then_inc(s_cb, 1)
                if front:
                    dve.wait_ge(s_cf, 4 * tn + 1)
                    nc.vector.scalar_tensor_tensor(out=y0, in0=y1, scalar=gate[:, 1, ds(tn, 1)], in1=y0,
                                                   op0=ALU.mult, op1=ALU.add).then_inc(s_cf, 1)
                if back:
                    dve.wait_ge(s_cb, 2 * t + 1)
                    nc.vector.tensor_scalar(z0, z0, mv[:, b, 0, 0:1], rstd[:, b, 0:1],
                                            ALU.subtract, ALU.mult).then_inc(s_cb, 1)
                if front:
                    dve.wait_ge(s_cf, 4 * tn + 2)
                    nc.vector.bn_stats(stats[:, f, 0, :], y0).then_inc(s_cf, 1)
                if back:
                    dve.wait_ge(s_cb, 2 * t + 2)
                    nc.vector.tensor_tensor(z1, z0, x1[:, ds(t, 1), :], ALU.add).then_inc(s_o, 1)
                if front:
                    dve.wait_ge(s_cf, 4 * tn + 3)
                    nc.vector.memset(pause[:, :], 0.0)
                    nc.vector.bn_aggr(mv[:, f, 0, :], stats[:, f, 0, :]).then_inc(s_cf, 1)
                    dve.wait_ge(s_cf, 4 * tn + 4)
                    nc.vector.tensor_scalar(mv[:, f, 0, 1:2], mv[:, f, 0, 1:2], EPS, None, ALU.add)\
                      .then_inc(s_var3, 1)

            combine(-1, NG - 1, True, False)
            if TT > NG:
                with dve.Fori(0, TT // NG - 1) as g:
                    for j in range(NG):
                        combine(NG * g + j, j, True, True)
            for j in range(NG):
                t = TT - NG + j
                combine(t, j, t + 1 < TT, True)


_INS = ['L0_attn_content', 'L0_attn_Wq', 'L0_attn_Wk', 'L0_attn_Wv', 'L0_ffn_router_w', 'L0_ffn_w_fc', 'L0_ffn_w_proj']


def kernel(**inputs):
    import numpy as _np
    import concourse.bacc as _bacc
    from concourse import mybir as _mybir
    from concourse.bass_utils import run_bass_kernel_spmd as _run

    nc = _bacc.Bacc("TRN2", target_bir_lowering=False, num_devices=1)
    arrays, args = {}, []
    for name in _INS:
        a = _np.ascontiguousarray(inputs[name])
        arrays[f"in_{name}"] = a
        args.append(nc.dram_tensor(f"in_{name}", a.shape, _mybir.dt.from_np(a.dtype), kind="ExternalInput").ap())
    shape = inputs[_INS[0]].shape
    args.append(nc.dram_tensor("out_0", shape, _mybir.dt.float32, kind="ExternalOutput").ap())
    sandwich(nc, *args)
    r = _run(nc, [arrays], core_ids=[0])
    return r.results[0]["out_0"]
```
